# Optimizing a Trainium2 kernel written in Bass

```python
import numpy as np
import jax
import jax.numpy as jnp

def _softmax(x, axis=-1):
    return jax.nn.softmax(x, axis=axis)

def _gelu(x):
    return jax.nn.gelu(x, approximate=True)

def _silu(x):
    return jax.nn.silu(x)

def _sigmoid(x):
    return jax.nn.sigmoid(x)

def _layernorm(x, axis=-1, eps=1e-05):
    m = jnp.mean(x, axis=axis, keepdims=True)
    v = jnp.var(x, axis=axis, keepdims=True)
    return (x - m) / jnp.sqrt(v + eps)

def _scatter_add(tgt, idx, src, axis=0):
    return tgt.at[idx].add(src)

def _segment_sum(src, seg, n):
    return jax.ops.segment_sum(src, seg, n)
kernel_name = 'mk_seq_preln_d2_jaxref_r8_7a4823'

def setup_inputs(seed: int=0):
    np.random.seed(seed)
    _w = jnp.asarray

    def _L0_attn_setup():
        import jax, jax.numpy as jnp
        import numpy as np
        import math
        DIM = 128
        N_HEADS = 16
        HEAD_DIM = DIM // N_HEADS

        def rope(x):
            S = x.shape[-2]
            D = x.shape[-1]
            pos = jnp.arange(S, dtype=x.dtype)[:, None]
            dim = jnp.arange(D // 2, dtype=x.dtype)[None, :]
            theta = pos / jnp.exp(2.0 * dim / D * math.log(10000.0))
            sin = jnp.sin(theta)[None, None]
            cos = jnp.cos(theta)[None, None]
            x1 = x[..., ::2]
            x2 = x[..., 1::2]
            out1 = x1 * cos - x2 * sin
            out2 = x1 * sin + x2 * cos
            return jnp.stack([out1, out2], axis=-1).reshape(x.shape)
        key = jax.random.key(seed)
        ks = jax.random.split(key, 9)
        B, S = (2, 256)
        s = 1.0 / math.sqrt(DIM)
        inp = {'x': jax.random.normal(ks[0], (B, S, DIM), dtype=jnp.float32), 'wq': jax.random.normal(ks[1], (DIM, DIM), dtype=jnp.float32) * s, 'bq': jnp.zeros((DIM,), dtype=jnp.float32), 'wk': jax.random.normal(ks[2], (DIM, DIM), dtype=jnp.float32) * s, 'bk': jnp.zeros((DIM,), dtype=jnp.float32), 'wv': jax.random.normal(ks[3], (DIM, DIM), dtype=jnp.float32) * s, 'bv': jnp.zeros((DIM,), dtype=jnp.float32), 'wo': jax.random.normal(ks[4], (DIM, DIM), dtype=jnp.float32) * s, 'bo': jnp.zeros((DIM,), dtype=jnp.float32)}
        return inp
    _L0_attn_in = _L0_attn_setup()

    def _L0_ffn_setup():
        import jax, jax.numpy as jnp
        import numpy as np
        B, T, C, H, E, K, F = (2, 256, 128, 16, 8, 2, 256)
        EPS = 1e-05

        def layernorm(x, w):
            m = x.mean(-1, keepdims=True)
            v = x.var(-1, keepdims=True)
            return (x - m) * jax.lax.rsqrt(v + EPS) * w

        def attention(x, c_attn_w, c_proj_w):
            b, t, c = x.shape
            hd = c // H
            q, k, v = jnp.split(x @ c_attn_w, 3, axis=-1)
            q = q.reshape(b, t, H, hd).transpose(0, 2, 1, 3)
            k = k.reshape(b, t, H, hd).transpose(0, 2, 1, 3)
            v = v.reshape(b, t, H, hd).transpose(0, 2, 1, 3)
            att = jnp.einsum('bhqd,bhkd->bhqk', q, k) / jnp.sqrt(jnp.asarray(hd, x.dtype))
            causal = jnp.tril(jnp.ones((t, t), bool))
            att = jnp.where(causal, att, jnp.asarray(-jnp.inf, att.dtype))
            att = jax.nn.softmax(att, axis=-1)
            y = jnp.einsum('bhqk,bhkd->bhqd', att, v)
            y = y.transpose(0, 2, 1, 3).reshape(b, t, c)
            return y @ c_proj_w

        def moe_mlp(x, router_w, w1, w2):
            b, t, c = x.shape
            xf = x.reshape(-1, c)
            router_logits = xf @ router_w
            probs = jax.nn.softmax(router_logits.astype(jnp.float32), axis=-1)
            rw, sel = jax.lax.top_k(probs, K)
            rw = rw / rw.sum(axis=-1, keepdims=True)
            rw = rw.astype(x.dtype)
            w1e = w1.reshape(c, E, F).transpose(1, 0, 2)
            w2e = w2.reshape(E, F, c)
            h = jax.nn.gelu(jnp.einsum('nc,ecf->enf', xf, w1e), approximate=False)
            y_all = jnp.einsum('enf,efc->nec', h, w2e)
            y_sel = jnp.take_along_axis(y_all, sel[:, :, None], axis=1)
            y = (y_sel * rw[:, :, None]).sum(axis=1)
            return y.reshape(b, t, c)
        key = jax.random.key(seed)
        ks = jax.random.split(key, 6)
        s = 0.02
        return {'x': jax.random.normal(ks[0], (B, T, C), jnp.float32), 'ln1_w': jnp.ones((C,), jnp.float32), 'c_attn_w': jax.random.normal(ks[1], (C, 3 * C), jnp.float32) * s, 'c_proj_w': jax.random.normal(ks[2], (C, C), jnp.float32) * s, 'ln2_w': jnp.ones((C,), jnp.float32), 'router_w': jax.random.normal(ks[3], (C, E), jnp.float32) * s, 'w1': jnp.clip(jax.random.normal(ks[4], (C, E * F), jnp.float32) * s, -0.06, 0.06), 'w2': jnp.clip(jax.random.normal(ks[5], (E * F, C), jnp.float32) * s, -0.06, 0.06)}
    _L0_ffn_in = _L0_ffn_setup()

    def _L1_attn_setup():
        import jax, jax.numpy as jnp
        import numpy as np
        B_, L_, E_ = (2, 256, 128)
        EXPAND, DSTATE, DCONV = (2, 16, 4)
        DIN = EXPAND * E_
        DTR = E_ // 16

        def _layer_norm(x, g, b, eps=1e-05):
            mu = jnp.mean(x, axis=-1, keepdims=True)
            var = jnp.mean(jnp.square(x - mu), axis=-1, keepdims=True)
            return (x - mu) * jax.lax.rsqrt(var + eps) * g + b

        def _mamba_forward(x, ln_g, ln_b, W_in, conv_w, conv_b, W_x, W_dt, dt_bias, A_log, D, W_out):
            L = x.shape[1]
            xn = _layer_norm(x, ln_g, ln_b)
            xz = jnp.einsum('ble,de->bld', xn, W_in)
            u, z = (xz[..., :DIN], xz[..., DIN:])
            up = jnp.pad(u, ((0, 0), (DCONV - 1, 0), (0, 0)))
            uc = conv_b
            uc = sum((conv_w[:, k] * up[:, k:k + L, :] for k in range(DCONV))) + conv_b
            u = jax.nn.silu(uc)
            dbc = jnp.einsum('bld,rd->blr', u, W_x)
            dt_in = dbc[..., :DTR]
            Bm = dbc[..., DTR:DTR + DSTATE]
            Cm = dbc[..., DTR + DSTATE:]
            dt = jax.nn.softplus(jnp.einsum('blr,dr->bld', dt_in, W_dt) + dt_bias)
            A = -jnp.exp(A_log)
            dA = jnp.exp(dt[..., None] * A)
            dBu = dt[..., None] * Bm[:, :, None, :] * u[..., None]

            def step(h, e):
                da, dbu, c = e
                h = da * h + dbu
                y = jnp.einsum('bdn,bn->bd', h, c)
                return (h, y)
            elems = (jnp.moveaxis(dA, 1, 0), jnp.moveaxis(dBu, 1, 0), jnp.moveaxis(Cm, 1, 0))
            h0 = jnp.zeros((x.shape[0], DIN, DSTATE), x.dtype)
            _, ys = jax.lax.scan(step, h0, elems)
            y = jnp.moveaxis(ys, 0, 1) + u * D
            y = y * jax.nn.silu(z)
            out = jnp.einsum('bld,ed->ble', y, W_out)
            return x + out
        key = jax.random.key(seed)
        ks = jax.random.split(key, 8)
        s = 0.02
        f32 = jnp.float32
        A_log = jnp.tile(jnp.log(jnp.arange(1, DSTATE + 1, dtype=f32)), (DIN, 1))
        return {'x': jax.random.normal(ks[0], (B_, L_, E_), f32), 'ln_g': jnp.ones((E_,), f32), 'ln_b': jnp.zeros((E_,), f32), 'W_in': jax.random.normal(ks[1], (2 * DIN, E_), f32) * s, 'conv_w': jax.random.normal(ks[2], (DIN, DCONV), f32) * s, 'conv_b': jnp.zeros((DIN,), f32), 'W_x': jax.random.normal(ks[3], (DTR + 2 * DSTATE, DIN), f32) * s, 'W_dt': jax.random.normal(ks[4], (DIN, DTR), f32) * s, 'dt_bias': jax.random.normal(ks[5], (DIN,), f32) * 0.01, 'A_log': A_log, 'D': jnp.ones((DIN,), f32), 'W_out': jax.random.normal(ks[6], (E_, DIN), f32) * s}
    _L1_attn_in = _L1_attn_setup()

    def _L1_ffn_setup():
        import jax, jax.numpy as jnp
        import numpy as np
        K_TOP = 4
        ALPHA = 1.702
        LIMIT = 7.0
        key = jax.random.key(seed)
        ks = jax.random.split(key, 4)
        B, S, H, E, inter = (2, 256, 128, 16, 128)
        return {'hidden_states': jax.random.normal(ks[0], (B, S, H), dtype=jnp.float32), 'router_weight': jax.random.normal(ks[1], (E, H), dtype=jnp.float32) * 0.02, 'router_bias': jnp.zeros((E,), dtype=jnp.float32), 'gate_up_proj': jax.random.normal(ks[2], (E, H, 2 * inter), dtype=jnp.float32) * 0.02, 'gate_up_bias': jnp.zeros((E, 2 * inter), dtype=jnp.float32), 'down_proj': jax.random.normal(ks[3], (E, inter, H), dtype=jnp.float32) * 0.02, 'down_bias': jnp.zeros((E, H), dtype=jnp.float32)}
    _L1_ffn_in = _L1_ffn_setup()
    _d = {'L0_attn_x': _L0_attn_in['x'], 'L0_attn_wq': _L0_attn_in['wq'], 'L0_attn_bq': _L0_attn_in['bq'], 'L0_attn_wk': _L0_attn_in['wk'], 'L0_attn_bk': _L0_attn_in['bk'], 'L0_attn_wv': _L0_attn_in['wv'], 'L0_attn_bv': _L0_attn_in['bv'], 'L0_attn_wo': _L0_attn_in['wo'], 'L0_attn_bo': _L0_attn_in['bo'], 'L0_ffn_ln1_w': _L0_ffn_in['ln1_w'], 'L0_ffn_c_attn_w': _L0_ffn_in['c_attn_w'], 'L0_ffn_c_proj_w': _L0_ffn_in['c_proj_w'], 'L0_ffn_ln2_w': _L0_ffn_in['ln2_w'], 'L0_ffn_router_w': _L0_ffn_in['router_w'], 'L0_ffn_w1': _L0_ffn_in['w1'], 'L0_ffn_w2': _L0_ffn_in['w2'], 'L1_attn_ln_g': _L1_attn_in['ln_g'], 'L1_attn_ln_b': _L1_attn_in['ln_b'], 'L1_attn_W_in': _L1_attn_in['W_in'], 'L1_attn_conv_w': _L1_attn_in['conv_w'], 'L1_attn_conv_b': _L1_attn_in['conv_b'], 'L1_attn_W_x': _L1_attn_in['W_x'], 'L1_attn_W_dt': _L1_attn_in['W_dt'], 'L1_attn_dt_bias': _L1_attn_in['dt_bias'], 'L1_attn_A_log': _L1_attn_in['A_log'], 'L1_attn_D': _L1_attn_in['D'], 'L1_attn_W_out': _L1_attn_in['W_out'], 'L1_ffn_router_weight': _L1_ffn_in['router_weight'], 'L1_ffn_router_bias': _L1_ffn_in['router_bias'], 'L1_ffn_gate_up_proj': _L1_ffn_in['gate_up_proj'], 'L1_ffn_gate_up_bias': _L1_ffn_in['gate_up_bias'], 'L1_ffn_down_proj': _L1_ffn_in['down_proj'], 'L1_ffn_down_bias': _L1_ffn_in['down_bias']}
    _x0 = _d['L0_attn_x']
    _d['L0_attn_x'] = jax.random.normal(jax.random.fold_in(jax.random.key(seed), 1), (32, 256, 128), dtype=_x0.dtype)
    del _x0
    return _d

def reference(L0_attn_x, L0_attn_wq, L0_attn_bq, L0_attn_wk, L0_attn_bk, L0_attn_wv, L0_attn_bv, L0_attn_wo, L0_attn_bo, L0_ffn_ln1_w, L0_ffn_c_attn_w, L0_ffn_c_proj_w, L0_ffn_ln2_w, L0_ffn_router_w, L0_ffn_w1, L0_ffn_w2, L1_attn_ln_g, L1_attn_ln_b, L1_attn_W_in, L1_attn_conv_w, L1_attn_conv_b, L1_attn_W_x, L1_attn_W_dt, L1_attn_dt_bias, L1_attn_A_log, L1_attn_D, L1_attn_W_out, L1_ffn_router_weight, L1_ffn_router_bias, L1_ffn_gate_up_proj, L1_ffn_gate_up_bias, L1_ffn_down_proj, L1_ffn_down_bias):

    def _L0_attn_ref(x, wq, bq, wk, bk, wv, bv, wo, bo):
        import jax, jax.numpy as jnp
        import numpy as np
        import math
        DIM = 128
        N_HEADS = 16
        HEAD_DIM = DIM // N_HEADS

        def rope(x):
            S = x.shape[-2]
            D = x.shape[-1]
            pos = jnp.arange(S, dtype=x.dtype)[:, None]
            dim = jnp.arange(D // 2, dtype=x.dtype)[None, :]
            theta = pos / jnp.exp(2.0 * dim / D * math.log(10000.0))
            sin = jnp.sin(theta)[None, None]
            cos = jnp.cos(theta)[None, None]
            x1 = x[..., ::2]
            x2 = x[..., 1::2]
            out1 = x1 * cos - x2 * sin
            out2 = x1 * sin + x2 * cos
            return jnp.stack([out1, out2], axis=-1).reshape(x.shape)
        B, S, _ = x.shape

        def proj(w, b):
            y = jnp.einsum('bsd,ed->bse', x, w) + b
            return y.reshape(B, S, N_HEADS, HEAD_DIM).transpose(0, 2, 1, 3)
        q = rope(proj(wq, bq))
        k = rope(proj(wk, bk))
        v = proj(wv, bv)
        score = jnp.einsum('bhqd,bhkd->bhqk', q, k) / math.sqrt(HEAD_DIM)
        causal = jnp.tril(jnp.ones((S, S), dtype=bool))
        score = jnp.where(causal[None, None], score, -jnp.inf)
        attn = jax.nn.softmax(score, axis=-1)
        out = jnp.einsum('bhqk,bhkd->bhqd', attn, v)
        out = out.transpose(0, 2, 1, 3).reshape(B, S, DIM)
        return jnp.einsum('bsd,ed->bse', out, wo) + bo

    def _L0_ffn_ref(x, ln1_w, c_attn_w, c_proj_w, ln2_w, router_w, w1, w2):
        import jax, jax.numpy as jnp
        import numpy as np
        B, T, C, H, E, K, F = (2, 256, 128, 16, 8, 2, 256)
        EPS = 1e-05

        def layernorm(x, w):
            m = x.mean(-1, keepdims=True)
            v = x.var(-1, keepdims=True)
            return (x - m) * jax.lax.rsqrt(v + EPS) * w

        def attention(x, c_attn_w, c_proj_w):
            b, t, c = x.shape
            hd = c // H
            q, k, v = jnp.split(x @ c_attn_w, 3, axis=-1)
            q = q.reshape(b, t, H, hd).transpose(0, 2, 1, 3)
            k = k.reshape(b, t, H, hd).transpose(0, 2, 1, 3)
            v = v.reshape(b, t, H, hd).transpose(0, 2, 1, 3)
            att = jnp.einsum('bhqd,bhkd->bhqk', q, k) / jnp.sqrt(jnp.asarray(hd, x.dtype))
            causal = jnp.tril(jnp.ones((t, t), bool))
            att = jnp.where(causal, att, jnp.asarray(-jnp.inf, att.dtype))
            att = jax.nn.softmax(att, axis=-1)
            y = jnp.einsum('bhqk,bhkd->bhqd', att, v)
            y = y.transpose(0, 2, 1, 3).reshape(b, t, c)
            return y @ c_proj_w

        def moe_mlp(x, router_w, w1, w2):
            b, t, c = x.shape
            xf = x.reshape(-1, c)
            router_logits = xf @ router_w
            probs = jax.nn.softmax(router_logits.astype(jnp.float32), axis=-1)
            rw, sel = jax.lax.top_k(probs, K)
            rw = rw / rw.sum(axis=-1, keepdims=True)
            rw = rw.astype(x.dtype)
            w1e = w1.reshape(c, E, F).transpose(1, 0, 2)
            w2e = w2.reshape(E, F, c)
            h = jax.nn.gelu(jnp.einsum('nc,ecf->enf', xf, w1e), approximate=False)
            y_all = jnp.einsum('enf,efc->nec', h, w2e)
            y_sel = jnp.take_along_axis(y_all, sel[:, :, None], axis=1)
            y = (y_sel * rw[:, :, None]).sum(axis=1)
            return y.reshape(b, t, c)
        x = x + attention(layernorm(x, ln1_w), c_attn_w, c_proj_w)
        x = x + moe_mlp(layernorm(x, ln2_w), router_w, w1, w2)
        return x

    def _L1_attn_ref(x, ln_g, ln_b, W_in, conv_w, conv_b, W_x, W_dt, dt_bias, A_log, D, W_out):
        import jax, jax.numpy as jnp
        import numpy as np
        B_, L_, E_ = (2, 256, 128)
        EXPAND, DSTATE, DCONV = (2, 16, 4)
        DIN = EXPAND * E_
        DTR = E_ // 16

        def _layer_norm(x, g, b, eps=1e-05):
            mu = jnp.mean(x, axis=-1, keepdims=True)
            var = jnp.mean(jnp.square(x - mu), axis=-1, keepdims=True)
            return (x - mu) * jax.lax.rsqrt(var + eps) * g + b

        def _mamba_forward(x, ln_g, ln_b, W_in, conv_w, conv_b, W_x, W_dt, dt_bias, A_log, D, W_out):
            L = x.shape[1]
            xn = _layer_norm(x, ln_g, ln_b)
            xz = jnp.einsum('ble,de->bld', xn, W_in)
            u, z = (xz[..., :DIN], xz[..., DIN:])
            up = jnp.pad(u, ((0, 0), (DCONV - 1, 0), (0, 0)))
            uc = conv_b
            uc = sum((conv_w[:, k] * up[:, k:k + L, :] for k in range(DCONV))) + conv_b
            u = jax.nn.silu(uc)
            dbc = jnp.einsum('bld,rd->blr', u, W_x)
            dt_in = dbc[..., :DTR]
            Bm = dbc[..., DTR:DTR + DSTATE]
            Cm = dbc[..., DTR + DSTATE:]
            dt = jax.nn.softplus(jnp.einsum('blr,dr->bld', dt_in, W_dt) + dt_bias)
            A = -jnp.exp(A_log)
            dA = jnp.exp(dt[..., None] * A)
            dBu = dt[..., None] * Bm[:, :, None, :] * u[..., None]

            def step(h, e):
                da, dbu, c = e
                h = da * h + dbu
                y = jnp.einsum('bdn,bn->bd', h, c)
                return (h, y)
            elems = (jnp.moveaxis(dA, 1, 0), jnp.moveaxis(dBu, 1, 0), jnp.moveaxis(Cm, 1, 0))
            h0 = jnp.zeros((x.shape[0], DIN, DSTATE), x.dtype)
            _, ys = jax.lax.scan(step, h0, elems)
            y = jnp.moveaxis(ys, 0, 1) + u * D
            y = y * jax.nn.silu(z)
            out = jnp.einsum('bld,ed->ble', y, W_out)
            return x + out
        return _mamba_forward(x, ln_g, ln_b, W_in, conv_w, conv_b, W_x, W_dt, dt_bias, A_log, D, W_out)

    def _L1_ffn_ref(hidden_states, router_weight, router_bias, gate_up_proj, gate_up_bias, down_proj, down_bias):
        import jax, jax.numpy as jnp
        import numpy as np
        K_TOP = 4
        ALPHA = 1.702
        LIMIT = 7.0
        B, S, H = hidden_states.shape
        E, inter, _ = down_proj.shape
        logits = jnp.einsum('bsh,eh->bse', hidden_states, router_weight) + router_bias
        scores = jax.nn.softmax(logits, axis=-1)
        topk_w, topk_i = jax.lax.top_k(scores, K_TOP)
        gu = jnp.einsum('bsh,ehn->bsen', hidden_states, gate_up_proj) + gate_up_bias
        gate = jnp.minimum(gu[..., :inter], LIMIT)
        up = jnp.clip(gu[..., inter:], -LIMIT, LIMIT)
        glu = gate * jax.nn.sigmoid(gate * ALPHA)
        activated = (up + 1.0) * glu
        down = jnp.einsum('bsek,ekh->bseh', activated, down_proj) + down_bias
        sel = jnp.take_along_axis(down, topk_i[..., None], axis=2)
        out = jnp.sum(sel * topk_w[..., None], axis=2)
        return out
    x = L0_attn_x
    x = x + _L0_attn_ref(_layernorm(x, axis=-1), L0_attn_wq, L0_attn_bq, L0_attn_wk, L0_attn_bk, L0_attn_wv, L0_attn_bv, L0_attn_wo, L0_attn_bo)
    x = x + _L0_ffn_ref(_layernorm(x, axis=-1), L0_ffn_ln1_w, L0_ffn_c_attn_w, L0_ffn_c_proj_w, L0_ffn_ln2_w, L0_ffn_router_w, L0_ffn_w1, L0_ffn_w2)
    x = x + _L1_attn_ref(_layernorm(x, axis=-1), L1_attn_ln_g, L1_attn_ln_b, L1_attn_W_in, L1_attn_conv_w, L1_attn_conv_b, L1_attn_W_x, L1_attn_W_dt, L1_attn_dt_bias, L1_attn_A_log, L1_attn_D, L1_attn_W_out)
    x = x + _L1_ffn_ref(_layernorm(x, axis=-1), L1_ffn_router_weight, L1_ffn_router_bias, L1_ffn_gate_up_proj, L1_ffn_gate_up_bias, L1_ffn_down_proj, L1_ffn_down_bias)
    return x

_drawn_inputs = setup_inputs


def setup_inputs(seed=0):
    import zlib

    import numpy as np

    out = dict(_drawn_inputs(seed))
    spreads = {'L0_attn_bq': (0.0, 0.482),
     'L0_attn_bk': (0.0, 0.598),
     'L0_attn_bv': (0.0, 0.1),
     'L0_attn_bo': (0.0, 0.1),
     'L0_ffn_ln1_w': (1.0, 0.6),
     'L0_ffn_ln2_w': (1.0, 0.6),
     'L1_attn_ln_g': (1.0, 0.6),
     'L1_attn_ln_b': (0.0, 0.8),
     'L1_attn_conv_b': (0.0, 0.8),
     'L1_attn_D': (1.0, 0.6),
     'L1_ffn_router_bias': (0.0, 0.8),
     'L1_ffn_gate_up_bias': (0.0, 0.8),
     'L1_ffn_down_bias': (0.0, 0.8)}
    factors = {'L0_ffn_c_attn_w': 7.987,
     'L0_ffn_c_proj_w': 7.977,
     'L0_ffn_router_w': 4.786,
     'L0_ffn_w1': 4.161,
     'L0_ffn_w2': 4.111,
     'L1_attn_W_in': 8.0,
     'L1_attn_conv_w': 8.0,
     'L1_attn_W_x': 8.0,
     'L1_attn_W_dt': 8.0,
     'L1_attn_dt_bias': 8.0,
     'L1_attn_A_log': 8.0,
     'L1_attn_W_out': 8.0,
     'L1_ffn_router_weight': 8.0,
     'L1_ffn_gate_up_proj': 8.0,
     'L1_ffn_down_proj': 8.0}
    for name, (base, spread) in spreads.items():
        noise = np.random.default_rng([zlib.crc32(name.encode()), seed]).standard_normal(out[name].shape)
        drawn = base * np.exp(spread * noise) if base else spread * noise
        out[name] = jnp.asarray(drawn.astype(out[name].dtype))
    for name, factor in factors.items():
        out[name] = (out[name] * factor).astype(out[name].dtype)
    return out
```

```python
from contextlib import ExitStack

import concourse.bass as bass
from concourse import mybir

ALU = mybir.AluOpType
ACT = mybir.ActivationFunctionType
AX = mybir.AxisListType
F32 = mybir.dt.float32
F32R = mybir.dt.float32r
BF16 = mybir.dt.bfloat16
U32 = mybir.dt.uint32

P = 128
C = 128
H = 16
HD = C // H
S = 256
NSEQ = 2
T = NSEQ * S
NT = T // P
NPART = 3
KS = NPART * NPART * HD
KM = KS + 2
SCALE = float(HD) ** -0.5
EPS = 1e-5
NEG = -3.0e38

E0, K0, F0 = 8, 2, 256
E1, K1, F1 = 16, 4, 128
ALPHA, LIMIT = 1.702, 7.0
DIN = 256
ND = DIN // P
NS = 16
NC = 4
NDT = C // 16
NCH = NS // 2


class Signal:

    def __init__(self, sem, per):
        self.sem, self.per, self.seen = sem, per, 0

    def at(self, it, k):
        assert 0 <= k <= self.per
        return self.sem, it * self.per + k


class Steps(Signal):

    def begin(self):
        self.seen = 0

    def note(self, ins):
        self.seen += 1
        assert self.seen <= self.per, "more steps than declared"
        ins.then_inc(self.sem, 1)

    def now(self, it):
        return self.at(it, self.seen)

    def end(self):
        assert self.seen == self.per, self.seen


class Ring:

    def __init__(self, bufs, full, free, uses, quiet=(), kept=()):
        self.bufs, self.full, self.free = bufs, full, free
        n = len(bufs)
        assert len(set(uses)) == len(uses)
        self.where = {u: (i % n, sum(1 for v in uses[i % n:i:n] if v not in kept)) for i, u in enumerate(uses)}
        self.per = [sum(1 for v in uses[b::n] if v not in kept) for b in range(n)]
        loud = [[u for i, u in enumerate(uses) if i % n == b and u not in quiet] for b in range(n)]
        self.rank = {u: k + 1 for line in loud for k, u in enumerate(line)}
        self.per_full = [len(line) for line in loud]

    def buf(self, use):
        return self.bufs[self.where[use][0]]

    def sem_full(self, use):
        return self.full[self.where[use][0]]

    def sem_free(self, use):
        return self.free[self.where[use][0]]

    def emptied(self, it, use):
        b, k = self.where[use]
        return self.free[b], it * self.per[b] + k

    def filled(self, it, use):
        b = self.where[use][0]
        return self.full[b], it * self.per_full[b] + self.rank[use]

    def filled_before(self, it):
        return self.full[0], it * self.per_full[0]

    def released(self, it, use):
        b, k = self.where[use]
        return self.free[b], it * self.per[b] + k + 1


INPUTS = [
    "x", "wqT", "wqsT", "wkT", "wksT", "wvT", "woT", "qk_bias", "bv", "bo", "cos", "sin",
    "ln1", "c_attn", "c_proj", "ln2", "router0", "w1", "w2",
    "ln_g", "ln_b", "WinT", "conv_w", "conv_b", "WxT", "WdtT", "dt_bias", "A_log", "D", "WoutT",
    "router1T", "router_bias", "gate_up", "gate_up_biasT", "down", "down_bias",
    "ident", "pick", "mask_qk", "mask_kq", "expert0", "expert1", "ones",
]

STEPS_DVE_A, STEPS_DVE_B, STEPS_ACT = 19, 34, 2
STACK_DMAS = 2 * NPART * NPART
W_READY = 15


def attention_uses(a):
    up = [("q", a), ("k", a)]
    smax = [[("max", a, s, g) for g in range(6)] for s in range(NSEQ)]
    probs = [[("st", a, s, g) for g in range(H // 2)] for s in range(NSEQ)]
    return (up + smax[0] + smax[1][:2] + [("mT", a, 0)] + smax[1][2:] + probs[0][:3] + [("mT", a, 1)]
            + probs[0][3:] + probs[1])


def build_program(nc, inp, out, pairs):
    x_dram = inp["x"].rearrange("(i n p) c -> i p n c", n=NT, p=P)
    out_dram = out.rearrange("(i n p) c -> i p n c", n=NT, p=P)

    ctx = ExitStack()
    with ctx:
        def sb(name, shape, dt=F32):
            return ctx.enter_context(nc.sbuf_tensor("sb_" + name, shape, dt))

        def sem(name):
            return ctx.enter_context(nc.semaphore(name))

        def signal(name, per):
            return Signal(sem(name), per)

        wq, wqs, wk, wks, wv, wo = (sb(n, [P, C]) for n in ("wq", "wqs", "wk", "wks", "wv", "wo"))
        qk_bias = sb("qk_bias", [P, 4])
        bv, bo = sb("bv", [P, C]), sb("bo", [P, C])
        cos, sin = sb("cos", [P, S]), sb("sin", [P, S])
        c_attn, c_proj = sb("c_attn", [P, 3 * C]), sb("c_proj", [P, C])
        ln1, ln2, ln_g, ln_b = (sb(n, [P, 1]) for n in ("ln1", "ln2", "ln_g", "ln_b"))
        router0, router1 = sb("router0", [P, E0]), sb("router1", [P, E1])
        w1h, w1l = sb("w1h", [P, E0 * F0], F32R), sb("w1l", [P, E0 * F0], F32R)
        w2 = sb("w2", [P, E0 * 2, C])
        win = sb("win", [P, 2 * DIN])
        conv_w, conv_b = sb("conv_w", [P, ND, NC]), sb("conv_b", [P, ND])
        wx = sb("wx", [P, ND, 2 * NS + NDT])
        wdt = sb("wdt", [2 * NS + NDT, DIN])
        dt_bias, skip = sb("dt_bias", [P, ND]), sb("skip", [P, ND])
        decay = sb("decay", [P, ND, NS])
        wout = sb("wout", [P, ND, C])
        router_bias = sb("router_bias", [P, E1])
        guh, gul = sb("guh", [P, E1, 2 * F1], F32R), sb("gul", [P, E1, 2 * F1], F32R)
        gu_bias = sb("gu_bias", [P, 2 * E1])
        down, down_bias = sb("down", [P, E1, C]), sb("down_bias", [E1, C])
        ident, identb = sb("ident", [P, P]), sb("identb", [P, P], BF16)
        mask_qk, mask_kq = sb("mask_qk", [P, P], BF16), sb("mask_kq", [P, P], BF16)
        expert0, expert1 = sb("expert0", [P, E0 * K0]), sb("expert1", [P, E1 * K1])
        pick = sb("pick", [NPART * 2 * NS, 2 * NS], BF16)
        minus_half = sb("minus_half", [P, NT])

        xin, xn, xnT = sb("xin", [P, NT, C]), sb("xn", [P, NT, C]), sb("xnT", [P, T])
        tmp = sb("tmp", [P, 4 * T])
        t1, t2, qf, kf = (tmp[:, i * T:(i + 1) * T] for i in range(4))
        parts = sb("parts", [P, 2, NPART, T], BF16)
        qs, ks = sb("qs", [P, H, T], BF16), sb("ks", [P, H, T], BF16)
        hid0 = qs[:].rearrange("p h t -> p (h t)").bitcast(F32)
        vaug = sb("vaug", [P, NT, H, HD + 1])
        mx = sb("mx", [P, NT, H])
        mparts = parts[0:H, 0, 0:2, :]
        recip = sb("recip", [P, 2 * H])
        x1, xa = sb("x1", [P, NT, C]), sb("xa", [P, NT, C])
        xfh, xfl = sb("xfh", [P, T], F32R), sb("xfl", [P, T], F32R)
        x2 = x1
        st_a, mv_a = sb("st_a", [P, NT, 6]), sb("mv_a", [P, NT, 2])
        ve_a, rstd_a = sb("ve_a", [P, NT]), sb("rstd_a", [P, NT])

        xl, ynT = sb("xl", [P, NT, C]), sb("ynT", [P, T])
        upad = sb("upad", [P, ND * NSEQ, NC - 1 + S])
        u = sb("u", [P, ND, T])
        dt = sb("dt", [P, ND, T])
        y = sb("y", [P, ND, 2, T])
        dtin = sb("dtin", [2 * NS + NDT, T])
        bcp = sb("bcp", [NPART * 2 * NS, T], BF16)
        bcr, bc2 = dtin[0:2 * NS, :], sb("bc2", [2 * NS, T], BF16)
        brow = sb("brow", [P, 2, T])
        da = sb("da", [P, 2, 2 * T])
        dbu = sb("dbu", [P, 2, 2 * T])
        hst = sb("hst", [P, 2, 2 * T])
        yhh, yhl = sb("yhh", [P, T], F32R), sb("yhl", [P, T], F32R)
        acc = sb("acc", [P, NT, C])
        st_b, mv_b = sb("st_b", [P, NT, 6]), sb("mv_b", [P, NT, 2])
        ve_b, rstd_b = sb("ve_b", [P, NT]), sb("rstd_b", [P, NT])
        zs = upad[:, :, NC - 1:NC - 1 + S]
        sp_x, sp_e = dbu[:, 0, :], dbu[:, 1, :]
        sp_w, sp_l = hst[:, 0, :], hst[:, 1, :]
        gate_b = [dbu[:, 0, 0:T], dbu[:, 0, T:2 * T]]
        tanh_b = [dbu[:, 1, 0:T], dbu[:, 1, T:2 * T]]
        up_b = [hst[:, 0, 0:T], hst[:, 0, T:2 * T]]
        act_bufs = [hst[:, 1, 0:T], hst[:, 1, T:2 * T]]

        def routing(name, e, k):
            return {"e": e, "k": k,
                    "ex": sb(name + "ex", [P, NT, e]), "m": sb(name + "m", [P, NT]),
                    "top": sb(name + "top", [P, NT, 8]), "idx": sb(name + "idx", [P, NT, 8], U32),
                    "idxf": sb(name + "idxf", [P, NT, 8]), "wk": sb(name + "wk", [P, NT, k]),
                    "r": sb(name + "r", [P, NT]), "hot": sb(name + "hot", [P, NT, e * k]),
                    "g": sb(name + "g", [P, NT, e]), "gh": sb(name + "gh", [P, NT, e])}

        ro0, ro1 = routing("ra_", E0, K0), routing("rb_", E1, K1)
        gT = dtin[0:E1, :]

        part_dram = nc.dram_tensor("part_scratch", (2, NPART, P, T), BF16, kind="Internal").ap()
        max_dram = nc.dram_tensor("max_scratch", (2, H, T), BF16, kind="Internal").ap()

        ps_sc = ctx.enter_context(nc.psum_tensor("ps_sc", [P, 2, 2 * T], F32))
        ps_am = ctx.enter_context(nc.psum_tensor("ps_am", [P, T], F32))
        ps_bc = ctx.enter_context(nc.psum_tensor("ps_bc", [P, 2 * T], F32))
        ps_bb = ctx.enter_context(nc.psum_tensor("ps_bb", [P, T], F32))

        def ring(name, bufs, uses, quiet=(), kept=()):
            return Ring(bufs, [sem(f"{name}_full{b}") for b in range(len(bufs))],
                        [sem(f"{name}_free{b}") for b in range(len(bufs))], uses, quiet, kept)

        sc = ring("sc", [ps_sc[:, b, :] for b in range(2)],
                  attention_uses(0) + attention_uses(1) + [("up", e) for e in range(E0)])
        am = ring("am", [ps_am[:, :]],
                  [(n, a) for a in range(2) for n in ("xT", "v", "pv0", "pv1", "oT", "proj")]
                  + ["xfT", "router"] + [("down", e) for e in range(E0)],
                  quiet=[(f"pv{s}", a) for s in range(NSEQ) for a in range(2)])
        bb = ring("bb", [ps_bb[:, :]],
                  ["ynT", "dbc"] + [("B", n) for n in range(NS)]
                  + ["out", "yhT", "router", "gT", "bias"] + [("down", e) for e in range(E1)])
        bc = ring("bc", [ps_bc[:, :]],
                  ["u", "z", "dt"] + [("C", g) for g in range(NCH)] + [("gu", e) for e in range(E1)],
                  kept=[("C", g) for g in range(NCH)])
        PROBS = [("st", a, s, g) for a in range(2) for s in range(NSEQ) for g in range(H // 2)]
        pr = ring("pr", [tmp[:, b * 768:(b + 1) * 768] for b in range(2)],
                  PROBS, quiet=PROBS)
        hid_bufs = [hid0[:, b * 2 * T:(b + 1) * 2 * T] for b in range(2)]
        chunks = [(g, d) for g in range(NCH) for d in range(ND)]
        dar = ring("dar", [da[:, b, :] for b in range(2)], chunks)
        dbr = ring("dbr", [dbu[:, b, :] for b in range(2)], chunks)
        hsr = ring("hsr", [hst[:, b, :] for b in range(2)], chunks)
        act_ready = signal("act_ready", E1)

        w_load = sem("w_load")
        w_ready = sem("w_ready")
        w_decay = sem("w_decay")
        x_loaded = signal("x_loaded", 16)
        var_a, rstd_s_a, norm_a = signal("var_a", 4), signal("rstd_s_a", 4), signal("norm_a", 4)
        var_b, rstd_s_b, norm_b = signal("var_b", 3), signal("rstd_s_b", 3), signal("norm_b", 3)
        qk_ready = signal("qk_ready", 2)
        p1_ready = signal("p1_ready", 4)
        rest_ready = signal("rest_ready", 2)
        p2_ready, p3_ready = signal("p2_ready", 4), signal("p3_ready", 4)
        parts_out = signal("parts_out", 2 * 16)
        stacked = signal("stacked", 2 * STACK_DMAS * 16)
        m1_ready = signal("m1_ready", 4)
        max_out, max_in = signal("max_out", 4 * 16), signal("max_in", 4 * 16)
        xbias_ready = signal("xbias_ready", 1)
        acc0_ready = signal("acc0_ready", 1)
        xf_ready, xfl_ready = signal("xf_ready", 1), signal("xfl_ready", 1)
        ex0_ready = signal("ex0_ready", 1)
        base_ready = signal("base_ready", 1)
        conv_ready, u_ready = signal("conv_ready", 1), signal("u_ready", 1)
        b1_ready, b2_ready, b2c_ready, b3_ready = (signal(n, 1) for n in ("b1_ready", "b2_ready", "b2c_ready", "b3_ready"))
        spe_ready, spw_ready, spl_ready = signal("spe_ready", 1), signal("spw_ready", 1), signal("spl_ready", 1)
        dt_ready, dtu_ready = signal("dt_ready", 1), signal("dtu_ready", 1)
        y_sum, y_skip, y_ready = signal("y_sum", 1), signal("y_skip", 1), signal("y_ready", 1)
        yhf_ready, yhl_ready = signal("yhf_ready", 1), signal("yhl_ready", 1)
        lg1_ready, ex1_ready, g1_ready = signal("lg1_ready", 1), signal("ex1_ready", 1), signal("g1_ready", 1)
        gate_ready, tanh_ready = signal("gate_ready", E1), signal("tanh_ready", E1)
        out_stored = signal("out_stored", 16)

        dve_a = Steps(sem("dve_a"), STEPS_DVE_A)
        dve_b = Steps(sem("dve_b"), STEPS_DVE_B)
        act_steps = Steps(sem("act_steps"), STEPS_ACT)

        raw_w1, raw_gu = da, (dbu, hst)
        W_RAW = [
            (raw_w1[:].rearrange("p a b -> p (a b)"), inp["w1"]),
            (raw_gu[0][:].rearrange("p a (e n) -> p (a e) n", n=2 * F1),
             inp["gate_up"][0:E1 // 2].rearrange("e h n -> h e n")),
            (raw_gu[1][:].rearrange("p a (e n) -> p (a e) n", n=2 * F1),
             inp["gate_up"][E1 // 2:E1].rearrange("e h n -> h e n")),
            (tmp[:, 0:P], inp["mask_qk"]), (tmp[:, P:2 * P], inp["mask_kq"]), (ident[:, :], inp["ident"]), (tmp[0:NPART * 2 * NS, 2 * P:2 * P + 2 * NS], inp["pick"]),
            (decay[:, :, :], inp["A_log"].rearrange("(d p) n -> p d n", p=P)),
        ]
        W_REST = [
            (ks[KS:KM, :, :], inp["ones"]),
            (wq[:, :], inp["wqT"]), (wqs[:, :], inp["wqsT"]), (wk[:, :], inp["wkT"]), (wks[:, :], inp["wksT"]),
            (wv[:, :], inp["wvT"]), (wo[:, :], inp["woT"]), (qk_bias[:, :], inp["qk_bias"]),
            (bv[:, :], inp["bv"]), (bo[:, :], inp["bo"]), (cos[:, :], inp["cos"]), (sin[:, :], inp["sin"]),
            (c_attn[:, :], inp["c_attn"]), (c_proj[:, :], inp["c_proj"]),
            (ln1[:, :], inp["ln1"]), (ln2[:, :], inp["ln2"]), (ln_g[:, :], inp["ln_g"]), (ln_b[:, :], inp["ln_b"]),
            (router0[:, :], inp["router0"]), (router1[:, :], inp["router1T"]),
            (w2[:, :, :], inp["w2"].rearrange("(k p) c -> p k c", p=P)),
            (win[:, :], inp["WinT"]),
            (conv_w[:, :, :], inp["conv_w"].rearrange("(d p) k -> p d k", p=P)),
            (conv_b[:, :], inp["conv_b"]),
            (wx[:, :, :], inp["WxT"].rearrange("(d p) r -> p d r", p=P)),
            (wdt[2 * NS:2 * NS + NDT, :], inp["WdtT"]),
            (dt_bias[:, :], inp["dt_bias"]),
            (skip[:, :], inp["D"]),
            (wout[:, :, :], inp["WoutT"].rearrange("(d p) c -> p d c", p=P)),
            (router_bias[:, :], inp["router_bias"]),
            (gu_bias[:, :], inp["gate_up_biasT"]),
            (down[:, :, :], inp["down"].rearrange("e f c -> f e c")),
            (down_bias[:, :], inp["down_bias"]),
            (expert0[:, :], inp["expert0"]), (expert1[:, :], inp["expert1"]),
        ]
        LOADS = 16 * (len(W_RAW) + len(W_REST))

        block = ctx.enter_context(nc.Block())

        @block.sync
        def _(sp):
            for dst, src in W_RAW + W_REST:
                sp.dma_start(dst, src).then_inc(w_load, 16)

            def counted(*marks):
                for _, value in marks:
                    sp.lower_val(value)
                return marks

            def pair(it, load_next):
                split = counted(*(p3_ready.at(it, 2 * a + 2) for a in range(2)))
                copied = counted(*(parts_out.at(it, 16 * (a + 1)) for a in range(2)))
                unused = counted(am.filled_before(it), pr.released(it, ("st", 0, NSEQ - 1, H // 2 - 1)))
                maxima = counted(*(sc.released(it, ("mT", a, s)) for a in range(2) for s in range(NSEQ)))
                max_copied = counted(*(max_out.at(it, 16 * (n + 1)) for n in range(2 * NSEQ)))
                xin_read = counted(norm_a.at(it, 1), xbias_ready.at(it, 1))
                finished, = counted(bb.released(it, ("down", E1 - 1)))

                for a in range(2):
                    sp.wait_ge(*split[a])
                    sp.dma_start(part_dram.rearrange("w i p t -> p w i t"), parts[:, :, :, :]).then_inc(parts_out.sem, 16)
                    sp.wait_ge(*copied[a])
                    sp.wait_ge(*unused[a])
                    for i in range(NPART):
                        for j in range(NPART):
                            row = (i * NPART + j) * HD
                            for w, part, dst in ((0, i, qs), (1, j, ks)):
                                sp.dma_start(dst[row:row + HD, :, :],
                                             part_dram[w, part].rearrange("(h d) t -> d h t", d=HD))\
                                  .then_inc(stacked.sem, 16)
                    if a == 0 and load_next:
                        for mark in xin_read:
                            sp.wait_ge(*mark)
                        sp.dma_start(xin[:, :, :], x_dram[it + 1]).then_inc(x_loaded.sem, 16)
                    for s in range(NSEQ):
                        cols = slice(s * S, (s + 1) * S)
                        sp.wait_ge(*maxima[NSEQ * a + s])
                        sp.dma_start(max_dram[:, :, cols].rearrange("i h t -> h i t"), mparts[:, :, cols])\
                          .then_inc(max_out.sem, 16)
                        sp.wait_ge(*max_copied[NSEQ * a + s])
                        sp.dma_start(qs[KS:KM, :, cols], max_dram[:, :, cols]).then_inc(max_in.sem, 16)
                sp.wait_ge(*finished)
                sp.dma_start(out_dram[it], acc[:, :, :]).then_inc(out_stored.sem, 16)

            sp.dma_start(xin[:, :, :], x_dram[0]).then_inc(x_loaded.sem, 16)
            pair(0, True)
            with sp.Fori(1, pairs - 1) as it:
                pair(it, True)
            pair(pairs - 1, False)
            sp.wait_ge(*out_stored.at(pairs, 0))

        @block.tensor
        def _(pe):
            mm, transpose = nc.tensor.matmul, nc.tensor.transpose

            def turn(src, dst):
                for t in range(NT):
                    last = transpose(dst[:, t * P:(t + 1) * P], src[:, t, :], ident[:, :])
                return last

            def attention(it, a):
                pe.wait_ge(*norm_a.at(it, 1 if a == 0 else 3))
                pe.wait_ge(*am.emptied(it, ("xT", a)))
                turn(xn, am.buf(("xT", a))).then_inc(am.sem_full(("xT", a)), 1)
                pe.wait_ge(*am.released(it, ("xT", a)))
                if a == 0:
                    for which, w, ws in (("q", wq, wqs), ("k", wk, wks)):
                        pe.wait_ge(*sc.emptied(it, (which, a)))
                        dst = sc.buf((which, a))
                        mm(dst[:, 0:T], w[:, :], xnT[:, :], start=True, stop=True)
                        mm(dst[:, T:2 * T], ws[:, :], xnT[:, :], start=True, stop=True)\
                            .then_inc(sc.sem_full((which, a)), 1)
                else:
                    for which, lo in (("q", 0), ("k", C)):
                        pe.wait_ge(*sc.emptied(it, (which, a)))
                        mm(sc.buf((which, a))[:, 0:T], c_attn[:, lo:lo + C], xnT[:, :], start=True, stop=True)\
                            .then_inc(sc.sem_full((which, a)), 1)
                pe.wait_ge(*am.emptied(it, ("v", a)))
                for t in range(NT):
                    last = mm(am.buf(("v", a))[:, t * P:(t + 1) * P], xnT[:, t * P:(t + 1) * P],
                              wv[:, :] if a == 0 else c_attn[:, 2 * C:3 * C], start=True, stop=True)
                last.then_inc(am.sem_full(("v", a)), 1)

                def max_pass(s, g):
                    use = ("max", a, s, g)
                    dst = sc.buf(use)
                    pe.wait_ge(*sc.emptied(it, use))
                    qt, heads, n = (1, range(4 * g, 4 * g + 4), S) if g < 4 else (0, range(8 * (g - 4), 8 * (g - 3)), P)
                    for j, h in enumerate(heads):
                        q0 = s * S + qt * P
                        mm(dst[:, (j + 1) * n - P:(j + 1) * n], identb[:, :], mask_qk[:, :],
                           start=True, stop=False, skip_group_check=True)
                        last = mm(dst[:, j * n:(j + 1) * n], qs[0:KS, h, q0:q0 + P], ks[0:KS, h, s * S:s * S + n],
                                  start=False, stop=True, skip_group_check=True)
                    last.then_inc(sc.sem_full(use), 1)

                def max_turn(s):
                    use = ("mT", a, s)
                    pe.wait_ge(*sc.emptied(it, use))
                    for g in (4, 5):
                        pe.wait_ge(*sc.released(it, ("max", a, s, g)))
                    for t in range(2):
                        last = transpose(sc.buf(use)[0:H, t * P:(t + 1) * P], mx[:, 2 * s + t, :], ident[:, :])
                    last.then_inc(sc.sem_full(use), 1)

                def scores(s, g):
                    use = ("st", a, s, g)
                    dst = sc.buf(use)
                    pe.wait_ge(*sc.emptied(it, use))
                    if g == 0:
                        pe.wait_ge(*max_in.at(it, 16 * (NSEQ * a + s + 1)))
                    for j in range(2):
                        h, s0 = 2 * g + j, s * S
                        mm(dst[:, j * S:j * S + P], identb[:, :], mask_kq[:, :],
                           start=True, stop=False, skip_group_check=True)
                        mm(dst[:, j * S:(j + 1) * S], ks[0:KM, h, s0:s0 + P], qs[0:KM, h, s0:s0 + S],
                           start=False, stop=True, skip_group_check=True)
                    for j in range(2):
                        h, s0 = 2 * g + j, s * S + P
                        cols = dst[:, 2 * S + j * P:2 * S + (j + 1) * P]
                        mm(cols, identb[:, :], mask_kq[:, :], start=True, stop=False)
                        last = mm(cols, ks[0:KM, h, s0:s0 + P], qs[0:KM, h, s0:s0 + P], start=False, stop=True)
                    last.then_inc(sc.sem_full(use), 1)

                def values(s, g):
                    use = ("st", a, s, g)
                    pv = am.buf((f"pv{s}", a))
                    if g == 0:
                        pe.wait_ge(*am.emptied(it, (f"pv{s}", a)))
                    if s == 0 and g == 0:
                        pe.wait_ge(*am.released(it, ("v", a)))
                    pe.wait_ge(*sc.released(it, use))
                    prob = pr.buf(use)
                    for j in range(2):
                        h = 2 * g + j
                        v0, v1 = vaug[:, 2 * s, h, :], vaug[:, 2 * s + 1, h, :]
                        o0, o1 = ((qt * H + h) * (HD + 1) for qt in range(2))
                        mm(pv[:, o0:o0 + HD + 1], prob[:, j * S:j * S + P], v0, start=True, stop=True)
                        mm(pv[:, o1:o1 + HD + 1], prob[:, j * S + P:(j + 1) * S], v0, start=True, stop=False)
                        last = mm(pv[:, o1:o1 + HD + 1], prob[:, 2 * S + j * P:2 * S + (j + 1) * P], v1,
                                  start=False, stop=True)
                    last.then_inc(pr.sem_free(use), 1)

                pe.wait_ge(*stacked.at(it, STACK_DMAS * 16 * (a + 1)))
                for g in range(6):
                    max_pass(0, g)
                for g in range(2):
                    max_pass(1, g)
                max_turn(0)
                for g in range(2, 6):
                    max_pass(1, g)
                for s in range(NSEQ):
                    for g in range(H // 2):
                        if s == 0 and g == 3:
                            max_turn(1)
                        scores(s, g)
                        if g >= 1:
                            values(s, g - 1)
                    values(s, H // 2 - 1)

                pe.wait_ge(*am.released(it, (f"pv{NSEQ - 1}", a)))
                pe.wait_ge(*am.emptied(it, ("oT", a)))
                turn(xn, am.buf(("oT", a))).then_inc(am.sem_full(("oT", a)), 1)
                pe.wait_ge(*am.released(it, ("oT", a)))
                pe.wait_ge(*am.emptied(it, ("proj", a)))
                for t in range(NT):
                    last = mm(am.buf(("proj", a))[:, t * P:(t + 1) * P], xnT[:, t * P:(t + 1) * P],
                              (wo if a == 0 else c_proj)[:, :], start=True, stop=True)
                last.then_inc(am.sem_full(("proj", a)), 1)

            def moe0(it):
                pe.wait_ge(*norm_a.at(it, 4))
                pe.wait_ge(*am.emptied(it, "xfT"))
                turn(xn, am.buf("xfT")).then_inc(am.sem_full("xfT"), 1)
                pe.wait_ge(*xf_ready.at(it, 1))
                pe.wait_ge(*am.emptied(it, "router"))
                for t in range(NT):
                    last = mm(am.buf("router")[:, t * E0:(t + 1) * E0], xnT[:, t * P:(t + 1) * P], router0[:, :],
                              start=True, stop=True)
                last.then_inc(am.sem_full("router"), 1)
                pe.wait_ge(*xfl_ready.at(it, 1))

                def up(e):
                    use = ("up", e)
                    pe.wait_ge(*sc.emptied(it, use))
                    for f in range(2):
                        dst = sc.buf(use)[:, f * T:(f + 1) * T]
                        cols = slice((2 * e + f) * P, (2 * e + f + 1) * P)
                        mm(dst, w1h[:, cols], xfh[:, :], start=True, stop=False)
                        mm(dst, w1h[:, cols], xfl[:, :], start=False, stop=False)
                        last = mm(dst, w1l[:, cols], xfh[:, :], start=False, stop=True)
                    last.then_inc(sc.sem_full(use), 1)

                def project(e):
                    pe.wait_ge(*sc.released(it, ("up", e)))
                    pe.wait_ge(*am.emptied(it, ("down", e)))
                    hid = hid_bufs[e % 2]
                    for t in range(NT):
                        for f in range(2):
                            last = mm(am.buf(("down", e))[:, t * P:(t + 1) * P],
                                      hid[:, f * T + t * P:f * T + (t + 1) * P], w2[:, 2 * e + f, :],
                                      start=(f == 0), stop=(f == 1))
                    last.then_inc(am.sem_full(("down", e)), 1)

                up(0)
                for e in range(E0):
                    if e + 1 < E0:
                        up(e + 1)
                    project(e)

            def mamba(it):
                pe.wait_ge(*norm_b.at(it, 2))
                pe.wait_ge(*bb.emptied(it, "ynT"))
                turn(acc, bb.buf("ynT")).then_inc(bb.sem_full("ynT"), 1)
                pe.wait_ge(*bb.released(it, "ynT"))
                for use, lo in (("u", 0), ("z", DIN)):
                    pe.wait_ge(*bc.emptied(it, use))
                    for d in range(ND):
                        last = mm(bc.buf(use)[:, d * T:(d + 1) * T], win[:, lo + d * P:lo + (d + 1) * P], ynT[:, :],
                                  start=True, stop=True)
                    last.then_inc(bc.sem_full(use), 1)
                pe.wait_ge(*u_ready.at(it, 1))
                pe.wait_ge(*bb.emptied(it, "dbc"))
                for d in range(ND):
                    last = mm(bb.buf("dbc")[0:2 * NS + NDT, :], wx[:, d, :], u[:, d, :], start=(d == 0), stop=(d == ND - 1))
                last.then_inc(bb.sem_full("dbc"), 1)
                pe.wait_ge(*b1_ready.at(it, 1))
                pe.wait_ge(*bc.emptied(it, "dt"))
                for d in range(ND):
                    last = mm(bc.buf("dt")[:, d * T:(d + 1) * T], wdt[2 * NS:2 * NS + NDT, d * P:(d + 1) * P],
                              dtin[2 * NS:2 * NS + NDT, :], start=True, stop=True)
                last.then_inc(bc.sem_full("dt"), 1)
                pe.wait_ge(*b2c_ready.at(it, 1))
                pe.wait_ge(*b3_ready.at(it, 1))

                def spread(dst, row):
                    return mm(dst, pick[:, row:row + 1].to_broadcast([NPART * 2 * NS, P]), bcp[:, :],
                              start=True, stop=True)

                for g in range(NCH):
                    for j in range(2):
                        n = 2 * g + j
                        pe.wait_ge(*bb.emptied(it, ("B", n)))
                        spread(bb.buf(("B", n)), n).then_inc(bb.sem_full(("B", n)), 1)
                    pe.wait_ge(*bc.emptied(it, ("C", g)))
                    if g >= 1:
                        pe.wait_ge(*hsr.filled(it, (g - 1, ND - 1)))
                    for j in range(2):
                        last = spread(bc.buf(("C", g))[:, j * T:(j + 1) * T], NS + 2 * g + j)
                    last.then_inc(bc.sem_full(("C", g)), 1)
                pe.wait_ge(*y_ready.at(it, 1))
                pe.wait_ge(*bb.emptied(it, "out"))
                for t in range(NT):
                    for d in range(ND):
                        last = mm(bb.buf("out")[:, t * P:(t + 1) * P], y[:, d, 0, t * P:(t + 1) * P], wout[:, d, :],
                                  start=(d == 0), stop=(d == ND - 1))
                last.then_inc(bb.sem_full("out"), 1)

            def moe1(it):
                pe.wait_ge(*norm_b.at(it, 3))
                pe.wait_ge(*bb.emptied(it, "yhT"))
                turn(acc, bb.buf("yhT")).then_inc(bb.sem_full("yhT"), 1)
                pe.wait_ge(*yhf_ready.at(it, 1))
                pe.wait_ge(*bb.emptied(it, "router"))
                for t in range(NT):
                    last = mm(bb.buf("router")[:, t * E1:(t + 1) * E1], ynT[:, t * P:(t + 1) * P], router1[:, :],
                              start=True, stop=True)
                last.then_inc(bb.sem_full("router"), 1)
                pe.wait_ge(*yhl_ready.at(it, 1))

                def gate_up(e):
                    use = ("gu", e)
                    pe.wait_ge(*bc.emptied(it, use))
                    for f in range(2):
                        dst = bc.buf(use)[:, f * T:(f + 1) * T]
                        cols = slice(f * F1, (f + 1) * F1)
                        mm(dst, guh[:, e, cols], yhh[:, :], start=True, stop=False)
                        mm(dst, guh[:, e, cols], yhl[:, :], start=False, stop=False)
                        last = mm(dst, gul[:, e, cols], yhh[:, :], start=False, stop=True)
                    last.then_inc(bc.sem_full(use), 1)

                def project(e):
                    pe.wait_ge(*act_ready.at(it, e + 1))
                    pe.wait_ge(*bb.emptied(it, ("down", e)))
                    for t in range(NT):
                        last = mm(bb.buf(("down", e))[:, t * P:(t + 1) * P], act_bufs[e % 2][:, t * P:(t + 1) * P],
                                  down[:, e, :], start=True, stop=True)
                    last.then_inc(bb.sem_full(("down", e)), 1)

                gate_up(0)
                pe.wait_ge(*g1_ready.at(it, 1))
                pe.wait_ge(*bb.emptied(it, "gT"))
                for t in range(NT):
                    last = transpose(bb.buf("gT")[0:E1, t * P:(t + 1) * P], ro1["g"][:, t, :], ident[:, :])
                last.then_inc(bb.sem_full("gT"), 1)
                pe.wait_ge(*bb.released(it, "gT"))
                pe.wait_ge(*bb.emptied(it, "bias"))
                for t in range(NT):
                    last = mm(bb.buf("bias")[:, t * P:(t + 1) * P], gT[:, t * P:(t + 1) * P], down_bias[:, :],
                              start=True, stop=True)
                last.then_inc(bb.sem_full("bias"), 1)
                for e in range(E1):
                    if e + 1 < E1:
                        gate_up(e + 1)
                    project(e)

            pe.wait_ge(w_load, LOADS)
            pe.wait_ge(w_ready, W_READY)
            def pair(it):
                attention(it, 0)
                attention(it, 1)
                moe0(it)
                mamba(it)
                moe1(it)

            pair(0)
            with pe.Fori(1, pairs) as it:
                pair(it)

        @block.vector
        def _(dve):
            V = nc.vector

            def layer_norm(it, steps, src, dst, stats, mv, ve, rstd, var, rstd_s, norm, k):
                for t in range(NT):
                    last = V.bn_stats(stats[:, t, :], src[:, t, :])
                steps.note(last)
                dve.wait_ge(*steps.now(it))
                V.memset(ve[:, :], 0.0)
                for t in range(NT):
                    last = V.bn_aggr(mv[:, t, :], stats[:, t, :])
                steps.note(last)
                dve.wait_ge(*steps.now(it))
                V.tensor_scalar(ve[:, :], mv[:, :, 1], EPS, None, ALU.add).then_inc(var.sem, 1)
                dve.wait_ge(*rstd_s.at(it, k + 1))
                for t in range(NT):
                    last = V.tensor_scalar(dst[:, t, :], src[:, t, :], mv[:, t, 0:1], rstd[:, t:t + 1],
                                           ALU.subtract, ALU.mult)
                last.then_inc(norm.sem, 1)

            def norm_of_a(it, k, src, dst):
                layer_norm(it, dve_a, src, dst, st_a, mv_a, ve_a, rstd_a, var_a, rstd_s_a, norm_a, k)

            def norm_of_b(it, k, src, dst):
                layer_norm(it, dve_b, src, dst, st_b, mv_b, ve_b, rstd_b, var_b, rstd_s_b, norm_b, k)

            def rope(it):
                for k, (which, dst) in enumerate((("q", qf), ("k", kf))):
                    use = (which, 0)
                    dve.wait_ge(*sc.filled(it, use))
                    if k == 1:
                        dve.wait_ge(*qk_ready.at(it, 1))
                    for lo, col, table, to in ((0, 2 * k, cos, t1), (T, 2 * k + 1, sin, t2)):
                        last = V.scalar_tensor_tensor(
                            out=to.rearrange("p (s t) -> p s t", s=NSEQ),
                            in0=sc.buf(use)[:, lo:lo + T].rearrange("p (s t) -> p s t", s=NSEQ),
                            scalar=qk_bias[:, col:col + 1],
                            in1=table[:, :].unsqueeze(1).to_broadcast([P, NSEQ, S]),
                            op0=ALU.add, op1=ALU.mult)
                    last.then_inc(sc.sem_free(use), 1)
                    dve.wait_ge(*sc.released(it, use))
                    V.tensor_tensor(dst, t1, t2, ALU.add).then_inc(qk_ready.sem, 1)

            def rests(it, a):
                for k, (which, dst) in enumerate((("q", qf), ("k", kf))):
                    dve.wait_ge(*p1_ready.at(it, 2 * a + k + 1))
                    if a == 0:
                        V.tensor_tensor(dst, dst, parts[:, k, 0, :], ALU.subtract).then_inc(rest_ready.sem, 1)
                    else:
                        V.tensor_tensor(dst, sc.buf((which, 1))[:, 0:T], parts[:, k, 0, :], ALU.subtract)\
                            .then_inc(sc.sem_free((which, 1)), 1)

            def take_values(it, a):
                use = ("v", a)
                dve.wait_ge(*am.filled(it, use))
                for t in range(NT):
                    v = am.buf(use)[:, t * P:(t + 1) * P].rearrange("p (h d) -> p h d", d=HD)
                    if a == 0:
                        last = V.tensor_tensor(vaug[:, t, :, 0:HD], v,
                                               bv[:, :].rearrange("p (h d) -> p h d", d=HD), ALU.add)
                    else:
                        last = V.tensor_copy(vaug[:, t, :, 0:HD], v)
                last.then_inc(am.sem_free(use), 1)

            def maximum(it, a, s, g):
                use = ("max", a, s, g)
                dve.wait_ge(*sc.filled(it, use))
                qt, h0, n = (1, 4 * g, S) if g < 4 else (0, 8 * (g - 4), P)
                V.tensor_reduce(mx[:, 2 * s + qt, h0:h0 + 2 * T // n], sc.buf(use).rearrange("p (h k) -> p h k", k=n),
                                AX.X, ALU.max, negate=True).then_inc(sc.sem_free(use), 1)

            def second_part(it, a, s):
                use = ("mT", a, s)
                dve.wait_ge(*sc.filled(it, use))
                dve.wait_ge(*m1_ready.at(it, NSEQ * a + s + 1))
                cols = slice(s * S, (s + 1) * S)
                V.tensor_tensor(mparts[:, 1, cols], sc.buf(use)[0:H, 0:S], mparts[:, 0, cols], ALU.subtract)\
                    .then_inc(sc.sem_free(use), 1)

            def normalise(it, a, s):
                use = (f"pv{s}", a)
                dve.wait_ge(*pr.released(it, ("st", a, s, H // 2 - 1)))
                pv = am.buf(use)[:, 0:2 * H * (HD + 1)].rearrange("p (h d) -> p h d", d=HD + 1)
                dve_a.note(V.reciprocal(recip[:, :], pv[:, :, HD]))
                dve.wait_ge(*dve_a.now(it))
                V.tensor_tensor(xn[:, 2 * s:2 * s + 2, :].rearrange("p t (h d) -> p (t h) d", d=HD), pv[:, :, 0:HD],
                                recip[:, :].unsqueeze(2).to_broadcast([P, 2 * H, HD]), ALU.mult)\
                    .then_inc(am.sem_free(use), 1)

            def attention(it, a):
                if a == 0:
                    rope(it)
                rests(it, a)
                take_values(it, a)
                for g in range(6):
                    maximum(it, a, 0, g)
                for g in range(2):
                    maximum(it, a, 1, g)
                second_part(it, a, 0)
                for g in range(2, 6):
                    maximum(it, a, 1, g)
                second_part(it, a, 1)
                for s in range(NSEQ):
                    normalise(it, a, s)

            def residual(it, dst, use, other):
                dve.wait_ge(*am.filled(it, use))
                V.tensor_tensor(dst[:, :, :], am.buf(use).rearrange("p (t c) -> p t c", c=C), other[:, :, :], ALU.add)\
                    .then_inc(am.sem_free(use), 1)
                dve.wait_ge(*am.released(it, use))

            def route(it, steps, ro, exp_ready, sums_all, done=None):
                e, k = ro["e"], ro["k"]
                dve.wait_ge(*exp_ready.at(it, 1))
                if sums_all:
                    V.tensor_reduce(ro["r"][:, :], ro["ex"][:, :, :], AX.X, ALU.add)
                else:
                    V.memset(ro["r"][:, :], 0.0)
                for t in range(NT):
                    last = V.max(ro["top"][:, t, :], ro["ex"][:, t, :])
                steps.note(last)
                dve.wait_ge(*steps.now(it))
                if sums_all:
                    V.reciprocal(ro["m"][:, :], ro["r"][:, :])
                else:
                    V.tensor_reduce(ro["r"][:, :], ro["top"][:, :, 0:k], AX.X, ALU.add)
                for t in range(NT):
                    last = V.max_index(ro["idx"][:, t, :], ro["top"][:, t, :], ro["ex"][:, t, :])
                steps.note(last)
                dve.wait_ge(*steps.now(it))
                if not sums_all:
                    V.reciprocal(ro["m"][:, :], ro["r"][:, :])
                steps.note(V.tensor_copy(ro["idxf"][:, :, :], ro["idx"][:, :, :]))
                dve.wait_ge(*steps.now(it))
                V.tensor_tensor(ro["wk"][:, :, :], ro["top"][:, :, 0:k],
                                ro["m"][:, :].unsqueeze(2).to_broadcast([P, NT, k]), ALU.mult)
                names = (expert0 if ro is ro0 else expert1)[:, :].rearrange("p (e k) -> p e k", k=k)
                for t in range(NT):
                    last = V.tensor_tensor(ro["hot"][:, t, :].rearrange("p (e k) -> p e k", k=k), names,
                                           ro["idxf"][:, t, 0:k].unsqueeze(1).to_broadcast([P, e, k]), ALU.is_equal)
                steps.note(last)
                dve.wait_ge(*steps.now(it))
                for t in range(NT):
                    last = V.tensor_tensor(ro["hot"][:, t, :].rearrange("p (e k) -> p e k", k=k),
                                           ro["hot"][:, t, :].rearrange("p (e k) -> p e k", k=k),
                                           ro["wk"][:, t, :].unsqueeze(1).to_broadcast([P, e, k]), ALU.mult)
                steps.note(last)
                dve.wait_ge(*steps.now(it))
                last = V.tensor_reduce(ro["g"][:, :, :].rearrange("p t e -> p (t e)"),
                                       ro["hot"][:, :, :].rearrange("p t (e k) -> p (t e) k", k=k), AX.X, ALU.add)
                if done is None:
                    steps.note(last)
                    dve.wait_ge(*steps.now(it))
                else:
                    last.then_inc(done.sem, 1)
                    dve.wait_ge(*done.at(it, 1))

            def weigh(it, line, use, gates, e, total):
                dve.wait_ge(*line.filled(it, use))
                for t in range(NT):
                    last = V.scalar_tensor_tensor(out=total[:, t, :], in0=line.buf(use)[:, t * P:(t + 1) * P],
                                                  scalar=gates[:, t, e:e + 1], in1=total[:, t, :],
                                                  op0=ALU.mult, op1=ALU.add)
                last.then_inc(line.sem_free(use), 1)

            def moe0(it):
                dve.wait_ge(*am.released(it, "xfT"))
                V.tensor_tensor(xfl[:, :], xnT[:, :], xfh[:, :], ALU.subtract).then_inc(xfl_ready.sem, 1)
                dve.wait_ge(*am.filled(it, "router"))
                logits = am.buf("router")[:, 0:NT * E0].rearrange("p (t e) -> p t e", e=E0)
                dve_a.note(V.tensor_reduce(ro0["m"][:, :], logits, AX.X, ALU.max))
                dve.wait_ge(*dve_a.now(it))
                V.tensor_tensor(ro0["ex"][:, :, :], logits, ro0["m"][:, :].unsqueeze(2).to_broadcast([P, NT, E0]),
                                ALU.subtract).then_inc(am.sem_free("router"), 1)
                route(it, dve_a, ro0, ex0_ready, False)
                dve.wait_ge(*acc0_ready.at(it, 1))
                for e in range(E0):
                    if e >= 1:
                        dve.wait_ge(*am.released(it, ("down", e - 1)))
                    weigh(it, am, ("down", e), ro0["g"], e, x2)
                dve.wait_ge(*am.released(it, ("down", E0 - 1)))

            def mamba(it):
                norm_of_b(it, 0, x2, xl)
                dve.wait_ge(*norm_b.at(it, 1))
                dve.wait_ge(*out_stored.at(it, 0))
                norm_of_b(it, 1, xl, acc)
                dve.wait_ge(*bc.released(it, "u"))
                for k in range(NC):
                    for d in range(ND):
                        src = upad[:, d * NSEQ:(d + 1) * NSEQ, k:k + S]
                        dst = u[:, d, :].rearrange("p (s t) -> p s t", s=NSEQ)
                        w = conv_w[:, d, k:k + 1]
                        if k == 0:
                            last = V.tensor_scalar(dst, src, w, conv_b[:, d:d + 1], ALU.mult, ALU.add)
                        else:
                            last = V.scalar_tensor_tensor(out=dst, in0=src, scalar=w, in1=dst,
                                                          op0=ALU.mult, op1=ALU.add)
                    if k < NC - 1:
                        dve_b.note(last)
                        dve.wait_ge(*dve_b.now(it))
                last.then_inc(conv_ready.sem, 1)
                dve.wait_ge(*b1_ready.at(it, 1))
                V.tensor_tensor(bcr[:, :], bb.buf("dbc")[0:2 * NS, :], bcp[0:2 * NS, :], ALU.subtract)\
                    .then_inc(bb.sem_free("dbc"), 1)
                dve.wait_ge(*b2_ready.at(it, 1))
                V.tensor_tensor(bcp[4 * NS:6 * NS, :], bcr[:, :], bc2[:, :], ALU.subtract).then_inc(b3_ready.sem, 1)
                dve.wait_ge(*u_ready.at(it, 1))
                for d in range(ND):
                    last = V.tensor_scalar(y[:, d, 0, :], u[:, d, :], skip[:, d:d + 1], None, ALU.mult)
                last.then_inc(y_skip.sem, 1)
                dve.wait_ge(*spe_ready.at(it, 1))
                V.tensor_scalar(sp_w, sp_e, 1.0, None, ALU.add).then_inc(spw_ready.sem, 1)
                dve.wait_ge(*spw_ready.at(it, 1))
                dve_b.note(V.scalar_tensor_tensor(out=sp_e, in0=sp_w, scalar=-1.0, in1=sp_e,
                                                  op0=ALU.add, op1=ALU.subtract))
                dve.wait_ge(*dve_b.now(it))
                dve_b.note(V.scalar_tensor_tensor(out=sp_x, in0=sp_x, scalar=0.0, in1=sp_e,
                                                  op0=ALU.max, op1=ALU.subtract))
                dve.wait_ge(*dve_b.now(it))
                dve.wait_ge(*spl_ready.at(it, 1))
                V.tensor_tensor(dt[:, :, :].rearrange("p d t -> p (d t)"), sp_x, sp_l, ALU.add)\
                    .then_inc(dt_ready.sem, 1)

                def scan(c):
                    use = chunks[c]
                    dve.wait_ge(*dar.filled(it, use))
                    dve.wait_ge(*dbr.filled(it, use))
                    dve.wait_ge(*hsr.emptied(it, use))
                    V.tensor_tensor_scan(hsr.buf(use), dar.buf(use), dbr.buf(use), 0.0, ALU.mult, ALU.add)\
                        .then_inc(dar.sem_free(use), 1)

                def times_c(c):
                    use = chunks[c]
                    g, d = use
                    dve.wait_ge(*dar.released(it, use))
                    if d == 0:
                        dve.wait_ge(*bc.filled(it, ("C", g)))
                    V.tensor_tensor(hsr.buf(use), hsr.buf(use), bc.buf(("C", g)), ALU.mult)\
                        .then_inc(hsr.sem_full(use), 1)

                scan(0)
                for c in range(len(chunks)):
                    if c + 1 < len(chunks):
                        scan(c + 1)
                    times_c(c)
                dve.wait_ge(*bb.filled(it, "out"))
                dve.wait_ge(*base_ready.at(it, 1))
                V.tensor_tensor(xl[:, :, :], bb.buf("out").rearrange("p (t c) -> p t c", c=C), xl[:, :, :], ALU.add)\
                    .then_inc(bb.sem_free("out"), 1)
                dve.wait_ge(*bb.released(it, "out"))

            def moe1(it):
                norm_of_b(it, 2, xl, acc)
                dve.wait_ge(*bb.released(it, "yhT"))
                V.tensor_tensor(yhl[:, :], ynT[:, :], yhh[:, :], ALU.subtract).then_inc(yhl_ready.sem, 1)
                dve.wait_ge(*bb.filled(it, "router"))
                V.tensor_tensor(ro1["ex"][:, :, :], bb.buf("router")[:, 0:NT * E1].rearrange("p (t e) -> p t e", e=E1),
                                router_bias[:, :].unsqueeze(1).to_broadcast([P, NT, E1]), ALU.add)\
                    .then_inc(bb.sem_free("router"), 1)
                dve.wait_ge(*bb.released(it, "router"))
                dve_b.note(V.tensor_reduce(ro1["m"][:, :], ro1["ex"][:, :, :], AX.X, ALU.max))
                dve.wait_ge(*dve_b.now(it))
                V.tensor_tensor(ro1["ex"][:, :, :], ro1["ex"][:, :, :],
                                ro1["m"][:, :].unsqueeze(2).to_broadcast([P, NT, E1]), ALU.subtract)\
                    .then_inc(lg1_ready.sem, 1)
                route(it, dve_b, ro1, ex1_ready, True, g1_ready)
                dve_b.note(V.tensor_scalar(ro1["gh"][:, :, :], ro1["g"][:, :, :], 0.5, None, ALU.mult))
                dve.wait_ge(*bb.filled(it, "bias"))
                V.tensor_tensor(acc[:, :, :], bb.buf("bias").rearrange("p (t c) -> p t c", c=C), xl[:, :, :], ALU.add)\
                    .then_inc(bb.sem_free("bias"), 1)
                dve.wait_ge(*bb.released(it, "bias"))

                def load_gate_up(e):
                    use, b = ("gu", e), e % 2
                    dve.wait_ge(*bc.filled(it, use))
                    V.tensor_scalar(gate_b[b], bc.buf(use)[:, 0:T], gu_bias[:, e:e + 1], LIMIT, ALU.add, ALU.min)\
                        .then_inc(gate_ready.sem, 1)
                    V.tensor_scalar(up_b[b], bc.buf(use)[:, T:2 * T], gu_bias[:, E1 + e:E1 + e + 1], LIMIT + 1,
                                    ALU.add, ALU.min).then_inc(bc.sem_free(use), 1)

                def activate(e):
                    b = e % 2
                    dve.wait_ge(*bc.released(it, ("gu", e)))
                    dve_b.note(V.scalar_tensor_tensor(out=up_b[b], in0=up_b[b], scalar=1.0 - LIMIT, in1=gate_b[b],
                                                      op0=ALU.max, op1=ALU.mult))
                    dve.wait_ge(*dve_b.now(it))
                    dve.wait_ge(*tanh_ready.at(it, e + 1))
                    if e >= 2:
                        dve.wait_ge(*bb.filled(it, ("down", e - 2)))
                    V.scalar_tensor_tensor(out=act_bufs[b], in0=tanh_b[b], scalar=1.0, in1=up_b[b],
                                           op0=ALU.add, op1=ALU.mult).then_inc(act_ready.sem, 1)

                for e in range(E1):
                    load_gate_up(e)
                    if e >= 1:
                        if e >= 2:
                            dve.wait_ge(*bb.released(it, ("down", e - 2)))
                        weigh(it, bb, ("down", e - 1), ro1["gh"], e - 1, acc)
                    activate(e)
                dve.wait_ge(*bb.released(it, ("down", E1 - 2)))
                weigh(it, bb, ("down", E1 - 1), ro1["gh"], E1 - 1, acc)

            dve.wait_ge(w_load, LOADS)
            raw0, raw1, raw2 = (r[:].rearrange("p a n -> p (a n)") for r in (da, dbu, hst))
            guh_f, gul_f = (g[:].rearrange("p e n -> p (e n)") for g in (guh, gul))
            half = E1 * F1
            splits = ((w1h[:, :], w1l[:, :], raw0), (guh_f[:, 0:half], gul_f[:, 0:half], raw1),
                      (guh_f[:, half:], gul_f[:, half:], raw2))
            for hi, _, raw in splits:
                V.tensor_copy(hi, raw).then_inc(w_ready, 1)
            V.tensor_copy(mask_qk[:, :], tmp[:, 0:P]).then_inc(w_ready, 1)
            V.tensor_copy(mask_kq[:, :], tmp[:, P:2 * P]).then_inc(w_ready, 1)
            V.tensor_copy(identb[:, :], ident[:, :]).then_inc(w_ready, 1)
            V.tensor_copy(pick[:, :], tmp[0:NPART * 2 * NS, 2 * P:2 * P + 2 * NS]).then_inc(w_ready, 1)
            V.memset(vaug[:, :, :, HD], 1.0).then_inc(w_ready, 1)
            V.memset(upad[:, :, 0:NC - 1], 0.0).then_inc(w_ready, 1)
            V.memset(minus_half[:, :], -0.5).then_inc(w_ready, 1)
            V.tensor_scalar(gu_bias[:, E1:2 * E1], gu_bias[:, E1:2 * E1], 1.0, None, ALU.add).then_inc(w_ready, 1)
            dve.wait_ge(w_ready, 3)
            for hi, lo, raw in splits:
                V.tensor_tensor(lo, raw, hi, ALU.subtract).then_inc(w_ready, 1)
            dve.wait_ge(w_ready, W_READY - 1)
            V.memset(da[:, :, :].rearrange("p b (j s) -> p (b j) s", s=S)[:, :, 0], 0.0).then_inc(w_ready, 1)

            def pair(it):
                dve_a.begin()
                dve_b.begin()
                dve.wait_ge(*x_loaded.at(it, 16))
                norm_of_a(it, 0, xin, xn)
                attention(it, 0)
                dve.wait_ge(*xbias_ready.at(it, 1))
                residual(it, x1, ("proj", 0), x1)
                norm_of_a(it, 1, x1, xa)
                dve.wait_ge(*norm_a.at(it, 2))
                norm_of_a(it, 2, xa, xn)
                attention(it, 1)
                residual(it, xa, ("proj", 1), xa)
                norm_of_a(it, 3, xa, xn)
                moe0(it)
                mamba(it)
                moe1(it)
                dve_a.end()
                dve_b.end()

            pair(0)
            with dve.Fori(1, pairs) as it:
                pair(it)

        @block.scalar
        def _(act):
            A = nc.scalar.activation

            def attention(it, a):
                use = ("xT", a)
                act.wait_ge(*am.filled(it, use))
                A(xnT[:, :], am.buf(use), ACT.Identity, scale=1.0 if a == 0 else ln1[:, 0:1])\
                    .then_inc(am.sem_free(use), 1)
                act.wait_ge(*parts_out.at(it, 16 * a))
                for k, (which, src) in enumerate((("q", qf), ("k", kf))):
                    if a == 0:
                        act.wait_ge(*qk_ready.at(it, k + 1))
                    else:
                        act.wait_ge(*sc.filled(it, (which, 1)))
                        src = sc.buf((which, 1))[:, 0:T]
                    A(parts[:, k, 0, :], src, ACT.Copy).then_inc(p1_ready.sem, 1)
                for k, (which, src) in enumerate((("q", qf), ("k", kf))):
                    if a == 0:
                        act.wait_ge(*rest_ready.at(it, k + 1))
                    else:
                        act.wait_ge(*sc.released(it, (which, 1)))
                    A(parts[:, k, 1, :], src, ACT.Copy).then_inc(p2_ready.sem, 1)

                def first_part(s):
                    use = ("mT", a, s)
                    act.wait_ge(*sc.filled(it, use))
                    A(mparts[:, 0, s * S:(s + 1) * S], sc.buf(use)[0:H, 0:S], ACT.Copy).then_inc(m1_ready.sem, 1)

                first_part(0)
                for s in range(NSEQ):
                    for g in range(H // 2):
                        if s == 0 and g == 3:
                            first_part(1)
                        use = ("st", a, s, g)
                        act.wait_ge(*sc.filled(it, use))
                        act.wait_ge(*pr.emptied(it, use))
                        A(pr.buf(use), sc.buf(use)[:, 0:768], ACT.Exp, scale=SCALE).then_inc(sc.sem_free(use), 1)
                use = ("oT", a)
                act.wait_ge(*am.filled(it, use))
                A(xnT[:, :], am.buf(use), ACT.Copy).then_inc(am.sem_free(use), 1)

            def moe0(it):
                act.wait_ge(*am.filled(it, "xfT"))
                A(xnT[:, :], am.buf("xfT"), ACT.Identity, scale=ln2[:, 0:1]).then_inc(xf_ready.sem, 1)
                A(xfh[:, :], am.buf("xfT"), ACT.Identity, scale=ln2[:, 0:1]).then_inc(am.sem_free("xfT"), 1)
                act.wait_ge(*am.released(it, "router"))
                A(ro0["ex"][:, :, :], ro0["ex"][:, :, :], ACT.Exp).then_inc(ex0_ready.sem, 1)
                for e in range(E0):
                    act.wait_ge(*sc.filled(it, ("up", e)))
                    if e >= 2:
                        act.wait_ge(*am.filled(it, ("down", e - 2)))
                    A(hid_bufs[e % 2], sc.buf(("up", e)), ACT.Gelu).then_inc(sc.sem_free(("up", e)), 1)

            def mamba(it):
                act.wait_ge(*bb.filled(it, "ynT"))
                A(ynT[:, :], bb.buf("ynT"), ACT.Identity, scale=ln_g[:, 0:1], bias=ln_b[:, 0:1])\
                    .then_inc(bb.sem_free("ynT"), 1)
                act.wait_ge(*bc.filled(it, "u"))
                act.wait_ge(*y_ready.at(it, 0))
                A(upad[:, :, NC - 1:NC - 1 + S], bc.buf("u").rearrange("p (d t) -> p d t", t=S), ACT.Copy)\
                    .then_inc(bc.sem_free("u"), 1)
                act.wait_ge(*conv_ready.at(it, 1))
                A(u[:, :, :], u[:, :, :], ACT.Silu).then_inc(u_ready.sem, 1)
                act.wait_ge(*bc.filled(it, "z"))
                A(zs, bc.buf("z").rearrange("p (d t) -> p d t", t=S), ACT.Silu).then_inc(bc.sem_free("z"), 1)
                act.wait_ge(*bb.filled(it, "dbc"))
                act_steps.note(A(dtin[2 * NS:2 * NS + NDT, :], bb.buf("dbc")[2 * NS:2 * NS + NDT, :], ACT.Copy))
                A(bcp[0:2 * NS, :], bb.buf("dbc")[0:2 * NS, :], ACT.Copy).then_inc(b1_ready.sem, 1)
                act.wait_ge(*bb.released(it, "dbc"))
                A(bc2[:, :], bcr[:, :], ACT.Copy).then_inc(b2_ready.sem, 1)
                A(bcp[2 * NS:4 * NS, :], bcr[:, :], ACT.Copy).then_inc(b2c_ready.sem, 1)
                act.wait_ge(*bc.filled(it, "dt"))
                for d in range(ND):
                    last = A(sp_x[:, d * T:(d + 1) * T], bc.buf("dt")[:, d * T:(d + 1) * T], ACT.Identity,
                             bias=dt_bias[:, d:d + 1])
                last.then_inc(bc.sem_free("dt"), 1)
                act.wait_ge(*bc.released(it, "dt"))
                act_steps.note(A(sp_e, sp_x, ACT.Abs))
                act.wait_ge(*act_steps.now(it))
                A(sp_e, sp_e, ACT.Exp, scale=-1.0).then_inc(spe_ready.sem, 1)
                act.wait_ge(*spw_ready.at(it, 1))
                A(sp_l, sp_w, ACT.Ln).then_inc(spl_ready.sem, 1)
                act.wait_ge(*dt_ready.at(it, 1))
                for g in range(NCH):
                    if g >= 1:
                        act.wait_ge(*dbr.filled(it, (g - 1, ND - 1)))
                    for j in range(2):
                        use = ("B", 2 * g + j)
                        act.wait_ge(*bb.filled(it, use))
                        A(brow[:, j, :], bb.buf(use), ACT.Copy).then_inc(bb.sem_free(use), 1)
                    for d in range(ND):
                        use = (g, d)
                        act.wait_ge(*dar.emptied(it, use))
                        for j in range(2):
                            last = A(dar.buf(use)[:, j * T:(j + 1) * T].rearrange("p (s t) -> p s t", s=NSEQ)[:, :, 1:S],
                                     dt[:, d, :].rearrange("p (s t) -> p s t", s=NSEQ)[:, :, 1:S],
                                     ACT.Exp, scale=decay[:, d, 2 * g + j:2 * g + j + 1])
                        last.then_inc(dar.sem_full(use), 1)

            def moe1(it):
                act.wait_ge(*bb.filled(it, "yhT"))
                A(ynT[:, :], bb.buf("yhT"), ACT.Copy).then_inc(yhf_ready.sem, 1)
                A(yhh[:, :], bb.buf("yhT"), ACT.Copy).then_inc(bb.sem_free("yhT"), 1)
                act.wait_ge(*lg1_ready.at(it, 1))
                A(ro1["ex"][:, :, :], ro1["ex"][:, :, :], ACT.Exp).then_inc(ex1_ready.sem, 1)
                act.wait_ge(*bb.filled(it, "gT"))
                A(gT[:, :], bb.buf("gT")[0:E1, :], ACT.Copy).then_inc(bb.sem_free("gT"), 1)
                for e in range(E1):
                    act.wait_ge(*gate_ready.at(it, e + 1))
                    if e >= 2:
                        act.wait_ge(*act_ready.at(it, e - 1))
                    A(tanh_b[e % 2], gate_b[e % 2], ACT.Tanh, scale=ALPHA / 2).then_inc(tanh_ready.sem, 1)

            act.wait_ge(w_load, LOADS)
            A(decay[:, :, :], decay[:, :, :], ACT.Exp).then_inc(w_decay, 1)
            act.wait_ge(w_decay, 1)
            A(decay[:, :, :], decay[:, :, :], ACT.Copy, scale=-1.0).then_inc(w_decay, 1)
            act.wait_ge(w_decay, 2)
            act.wait_ge(w_ready, W_READY)
            def pair(it):
                act_steps.begin()
                attention(it, 0)
                attention(it, 1)
                moe0(it)
                mamba(it)
                moe1(it)
                act_steps.end()

            pair(0)
            with act.Fori(1, pairs) as it:
                pair(it)

        @block.gpsimd
        def _(pool):
            G = nc.gpsimd.tensor_tensor

            def power(it, k, ve, rstd, var, rstd_s):
                pool.wait_ge(*var.at(it, k + 1))
                G(rstd[:, :], ve[:, :], minus_half[:, :], ALU.pow).then_inc(rstd_s.sem, 1)

            def third_parts(it, a):
                for k, src in enumerate((qf, kf)):
                    pool.wait_ge(*p2_ready.at(it, 2 * a + k + 1))
                    G(parts[:, k, 2, :], src, parts[:, k, 1, :], ALU.subtract).then_inc(p3_ready.sem, 1)

            def thread_a(it):
                power(it, 0, ve_a, rstd_a, var_a, rstd_s_a)
                pool.wait_ge(*x_loaded.at(it, 16))
                G(x1[:, :, :], xin[:, :, :], bo[:, :].unsqueeze(1).to_broadcast([P, NT, C]), ALU.add)\
                    .then_inc(xbias_ready.sem, 1)
                third_parts(it, 0)
                power(it, 1, ve_a, rstd_a, var_a, rstd_s_a)
                power(it, 2, ve_a, rstd_a, var_a, rstd_s_a)
                third_parts(it, 1)
                power(it, 3, ve_a, rstd_a, var_a, rstd_s_a)
                pool.wait_ge(*am.released(it, ("proj", 1)))
                G(x2[:, :, :], x1[:, :, :], xa[:, :, :], ALU.add).then_inc(acc0_ready.sem, 1)

            def mamba(it):
                power(it, 0, ve_b, rstd_b, var_b, rstd_s_b)
                power(it, 1, ve_b, rstd_b, var_b, rstd_s_b)
                pool.wait_ge(*norm_b.at(it, 2))
                G(xl[:, :, :], x2[:, :, :], xl[:, :, :], ALU.add).then_inc(base_ready.sem, 1)
                pool.wait_ge(*dt_ready.at(it, 1))
                pool.wait_ge(*u_ready.at(it, 1))
                pool.wait_ge(*y_skip.at(it, 1))
                G(u[:, :, :], dt[:, :, :], u[:, :, :], ALU.mult).then_inc(dtu_ready.sem, 1)
                pool.wait_ge(*dtu_ready.at(it, 1))

                def dt_b_u(c):
                    use = chunks[c]
                    g, d = use
                    if d == 0:
                        pool.wait_ge(*bb.released(it, ("B", 2 * g + 1)))
                    if c >= 2:
                        pool.wait_ge(*dar.released(it, chunks[c - 2]))
                    G(dbr.buf(use).rearrange("p (j t) -> p j t", j=2), brow[:, :, :],
                      u[:, d, :].unsqueeze(1).to_broadcast([P, 2, T]), ALU.mult).then_inc(dbr.sem_full(use), 1)

                def add_y(c):
                    use = chunks[c]
                    g, d = use
                    pool.wait_ge(*hsr.filled(it, use))
                    if g >= 1:
                        pool.wait_ge(*hsr.released(it, chunks[c - 2]))
                    h2 = hsr.buf(use).rearrange("p (j t) -> p j t", j=2)
                    if g == 0:
                        G(y[:, d, 0, :], y[:, d, 0, :], h2[:, 0, :], ALU.add)
                        ins = nc.gpsimd.tensor_copy(y[:, d, 1, :], h2[:, 1, :])
                    else:
                        ins = G(y[:, d, :, :], y[:, d, :, :], h2, ALU.add)
                    ins.then_inc(hsr.sem_free(use), 1)

                dt_b_u(0)
                for c in range(len(chunks)):
                    if c + 1 < len(chunks):
                        dt_b_u(c + 1)
                    add_y(c)
                pool.wait_ge(*hsr.released(it, chunks[-1]))
                pool.wait_ge(*hsr.released(it, chunks[-2]))
                G(y[:, :, 0, :], y[:, :, 0, :], y[:, :, 1, :], ALU.add).then_inc(y_sum.sem, 1)
                pool.wait_ge(*y_sum.at(it, 1))
                pool.wait_ge(*bc.released(it, "z"))
                G(y[:, :, 0, :].rearrange("p d (s t) -> p d s t", s=NSEQ), y[:, :, 0, :].rearrange("p d (s t) -> p d s t", s=NSEQ),
                  zs.rearrange("p (d s) t -> p d s t", s=NSEQ), ALU.mult).then_inc(y_ready.sem, 1)

            pool.wait_ge(w_load, LOADS)
            pool.wait_ge(w_ready, W_READY)
            def pair(it):
                thread_a(it)
                mamba(it)
                power(it, 2, ve_b, rstd_b, var_b, rstd_s_b)

            pair(0)
            with pool.Fori(1, pairs) as it:
                pair(it)


def _swap_pairs(w):
    return w.reshape(C // 2, 2, -1)[:, ::-1].reshape(w.shape)


def _constants(np):
    pos = np.arange(S, dtype=np.float32)[:, None]
    dim = np.arange(HD // 2, dtype=np.float32)[None, :]
    theta = pos / np.exp(np.float32(2.0) * dim / np.float32(HD) * np.float32(np.log(10000.0)))
    cos, sin = np.cos(theta), np.sin(theta)
    sign = np.array([-1.0, 1.0], np.float32)
    cosT = np.repeat(cos.T, 2, axis=0)
    sinT = np.repeat(sin.T, 2, axis=0) * np.tile(sign, HD // 2)[:, None]
    i = np.arange(P)
    later = i[None, :] > i[:, None]
    one = np.arange(2 * NS)
    return {
        "cos": np.tile(cosT, (H, 1)).astype(np.float32), "sin": np.tile(sinT, (H, 1)).astype(np.float32),
        "ident": np.eye(P, dtype=np.float32),
        "pick": np.tile((one[:, None] == one[None, :]).astype(np.float32), (NPART, 1)),
        "mask_qk": np.where(later, np.float32(NEG), np.float32(0)).astype(np.float32),
        "mask_kq": np.where(later.T, np.float32(NEG), np.float32(0)).astype(np.float32),
        "expert0": np.tile(np.repeat(np.arange(E0, dtype=np.float32), K0), (P, 1)),
        "expert1": np.tile(np.repeat(np.arange(E1, dtype=np.float32), K1), (P, 1)),
        "ones": np.ones((KM - KS, H, T), mybir.dt.np(BF16)),
    }


def kernel(**inputs):
    import numpy as np
    import concourse.bacc as bacc
    from concourse.bass_utils import run_bass_kernel_spmd

    i = {k: np.asarray(v) for k, v in inputs.items()}
    a, f, m, g = "L0_attn_", "L0_ffn_", "L1_attn_", "L1_ffn_"
    x = i[a + "x"]
    n_seq = x.shape[0]
    wx, gub = i[m + "W_x"], i[g + "gate_up_bias"]
    arrays = {
        "x": x.reshape(-1, C),
        "wqT": i[a + "wq"].T, "wqsT": _swap_pairs(i[a + "wq"]).T,
        "wkT": i[a + "wk"].T, "wksT": _swap_pairs(i[a + "wk"]).T,
        "wvT": i[a + "wv"].T, "woT": i[a + "wo"].T,
        "qk_bias": np.stack([i[a + "bq"], _swap_pairs(i[a + "bq"]), i[a + "bk"], _swap_pairs(i[a + "bk"])], axis=1),
        "bv": np.tile(i[a + "bv"], (P, 1)), "bo": np.tile(i[a + "bo"], (P, 1)),
        "ln1": i[f + "ln1_w"][:, None], "ln2": i[f + "ln2_w"][:, None],
        "c_attn": i[f + "c_attn_w"], "c_proj": i[f + "c_proj_w"],
        "router0": i[f + "router_w"], "w1": i[f + "w1"], "w2": i[f + "w2"],
        "ln_g": i[m + "ln_g"][:, None], "ln_b": i[m + "ln_b"][:, None],
        "WinT": i[m + "W_in"].T, "conv_w": i[m + "conv_w"], "conv_b": i[m + "conv_b"].reshape(ND, P).T,
        "WxT": np.concatenate([wx[NDT:], wx[:NDT]]).T, "WdtT": i[m + "W_dt"].T,
        "dt_bias": i[m + "dt_bias"].reshape(ND, P).T, "A_log": i[m + "A_log"], "D": i[m + "D"].reshape(ND, P).T, "WoutT": i[m + "W_out"].T,
        "router1T": i[g + "router_weight"].T, "router_bias": np.tile(i[g + "router_bias"], (P, 1)),
        "gate_up": i[g + "gate_up_proj"],
        "gate_up_biasT": np.concatenate([gub[:, :F1], gub[:, F1:]]).T,
        "down": i[g + "down_proj"], "down_bias": i[g + "down_bias"],
        **_constants(np),
    }
    assert set(arrays) == set(INPUTS)
    nc = bacc.Bacc("TRN2", target_bir_lowering=False, num_devices=1)
    feed, aps = {}, {}
    for name in INPUTS:
        arr = np.ascontiguousarray(arrays[name])
        feed[f"in_{name}"] = arr
        aps[name] = nc.dram_tensor(f"in_{name}", arr.shape, mybir.dt.from_np(arr.dtype), kind="ExternalInput").ap()
    out = nc.dram_tensor("out_y", (n_seq * S, C), F32, kind="ExternalOutput").ap()
    build_program(nc, aps, out, n_seq // NSEQ)
    r = run_bass_kernel_spmd(nc, [feed], core_ids=[0])
    return r.results[0]["out_y"].reshape(n_seq, S, C)
```

```python
from contextlib import ExitStack

import concourse.bass as bass
from concourse import mybir

ALU = mybir.AluOpType
ACT = mybir.ActivationFunctionType
AX = mybir.AxisListType
F32 = mybir.dt.float32
F32R = mybir.dt.float32r
BF16 = mybir.dt.bfloat16
U32 = mybir.dt.uint32

P = 128
C = 128
H = 16
HD = C // H
S = 256
NSEQ = 2
T = NSEQ * S
NT = T // P
NPART = 3
KS = NPART * NPART * HD
STRIP = 32
KM = KS + 2
SCALE = float(HD) ** -0.5
EPS = 1e-5
NEG = -3.0e38

E0, K0, F0 = 8, 2, 256
E1, K1, F1 = 16, 4, 128
ALPHA, LIMIT = 1.702, 7.0
DIN = 256
ND = DIN // P
NS = 16
NC = 4
NDT = C // 16
NCH = NS // 2


class Signal:

    def __init__(self, sem, per):
        self.sem, self.per, self.seen = sem, per, 0

    def at(self, it, k):
        assert 0 <= k <= self.per
        return self.sem, it * self.per + k


def steps_of(a, b):
    def front(step, *args):
        if a is not None:
            step(a, *args)

    def back(step, *args):
        if b is not None:
            step(b, *args)
    return front, back


class Steps(Signal):

    def begin(self):
        self.seen = 0

    def note(self, ins):
        self.seen += 1
        assert self.seen <= self.per, "more steps than declared"
        ins.then_inc(self.sem, 1)

    def now(self, it):
        return self.at(it, self.seen)

    def end(self):
        assert self.seen == self.per, self.seen


class Ring:

    def __init__(self, bufs, full, free, uses, quiet=(), kept=()):
        self.bufs, self.full, self.free = bufs, full, free
        n = len(bufs)
        assert len(set(uses)) == len(uses)
        self.where = {u: (i % n, sum(1 for v in uses[i % n:i:n] if v not in kept)) for i, u in enumerate(uses)}
        self.per = [sum(1 for v in uses[b::n] if v not in kept) for b in range(n)]
        loud = [[u for i, u in enumerate(uses) if i % n == b and u not in quiet] for b in range(n)]
        self.rank = {u: k + 1 for line in loud for k, u in enumerate(line)}
        self.per_full = [len(line) for line in loud]

    def buf(self, use):
        return self.bufs[self.where[use][0]]

    def sem_full(self, use):
        return self.full[self.where[use][0]]

    def sem_free(self, use):
        return self.free[self.where[use][0]]

    def emptied(self, it, use):
        b, k = self.where[use]
        return self.free[b], it * self.per[b] + k

    def filled(self, it, use):
        b = self.where[use][0]
        return self.full[b], it * self.per_full[b] + self.rank[use]

    def released(self, it, use):
        b, k = self.where[use]
        return self.free[b], it * self.per[b] + k + 1


INPUTS = [
    "x", "wqT", "wqsT", "wkT", "wksT", "wvT", "woT", "qk_bias", "bv", "bo", "cos", "sin",
    "ln1", "c_attn", "c_proj", "ln2", "router0", "w1", "w2",
    "ln_g", "ln_b", "WinT", "conv_w", "conv_b", "WxT", "WdtT", "dt_bias", "A_log", "D", "WoutT",
    "router1T", "router_bias", "gate_up", "gate_up_biasT", "down", "down_bias",
    "ident", "pick", "mask_qk", "mask_kq", "expert0", "expert1", "ones",
]

STEPS_DVE_A, STEPS_DVE_B, STEPS_ACT = 16, 40, 2
PART_DMAS = STACK_DMAS = 2 * NPART
W_READY = 15


SCORES_AT = [[6, 7], [8, 9], [10, 11], [12, 13], [14, 15]] + [[]] * (2 * NCH - 5)
OUT_AT, NEXT_AT = 5, 10
ATTEND_AT = [[2], [3], [4], [5, 6], [7], [8], [9], [10], [11], [12], [13], [14], [15]] + [[]] * (E1 - 13)
OUT1_AT = 13
DVE_CHUNKS = range(1, 2 * NCH, 2)


def normalised(steps):
    turned = {5: (0, 0), H // 2 + 1: (0, 1), H // 2 + 5: (1, 0)}
    return [turned[n] for n in steps if n in turned]


def attention_uses(a):
    up = [("q", a), ("k", a)]
    smax = [[("max", a, s, g) for g in range(6)] for s in range(NSEQ)]
    probs = [[("st", a, s, g) for g in range(H // 2)] for s in range(NSEQ)]
    vt = [[("vT", a, s, half) for half in range(2)] for s in range(NSEQ)]
    return (up + smax[0] + smax[1][:2] + [("mT", a, 0)] + smax[1][2:] + [("mT", a, 1)]
            + probs[0][:6] + [vt[0][0]] + probs[0][6:] + probs[1][:2] + [vt[0][1]] + probs[1][2:6]
            + [vt[1][0]] + probs[1][6:] + [vt[1][1]])


def build_program(nc, inp, out, pairs):
    x_dram = inp["x"].rearrange("(i n p) c -> i p n c", n=NT, p=P)
    out_dram = out.rearrange("(i n p) c -> i p n c", n=NT, p=P)

    ctx = ExitStack()
    with ctx:
        def sb(name, shape, dt=F32):
            return ctx.enter_context(nc.sbuf_tensor("sb_" + name, shape, dt))

        def sem(name):
            return ctx.enter_context(nc.semaphore(name))

        def signal(name, per):
            return Signal(sem(name), per)

        wq, wqs, wk, wks, wv, wo = (sb(n, [P, C]) for n in ("wq", "wqs", "wk", "wks", "wv", "wo"))
        qk_bias = sb("qk_bias", [P, 4])
        bv, bo = sb("bv", [P, C]), sb("bo", [P, C])
        cos, sin = sb("cos", [P, S]), sb("sin", [P, S])
        c_attn, c_proj = sb("c_attn", [P, 3 * C]), sb("c_proj", [P, C])
        ln1, ln2, ln_g, ln_b = (sb(n, [P, 1]) for n in ("ln1", "ln2", "ln_g", "ln_b"))
        router0, router1 = sb("router0", [P, E0]), sb("router1", [P, E1])
        w1h, w1l = sb("w1h", [P, E0 * F0], F32R), sb("w1l", [P, E0 * F0], F32R)
        w2 = sb("w2", [P, E0 * 2, C])
        win = sb("win", [P, 2 * DIN])
        conv_w, conv_b = sb("conv_w", [P, ND, NC]), sb("conv_b", [P, ND])
        wx = sb("wx", [P, ND, 2 * NS + NDT])
        wdt = sb("wdt", [2 * NS + NDT, DIN])
        dt_bias, skip = sb("dt_bias", [P, ND]), sb("skip", [P, ND])
        decay = sb("decay", [P, ND, NS])
        wout = sb("wout", [P, ND, C])
        router_bias = sb("router_bias", [P, E1])
        guh, gul = sb("guh", [P, E1, 2 * F1], F32R), sb("gul", [P, E1, 2 * F1], F32R)
        gu_bias = sb("gu_bias", [P, 2 * E1])
        down, down_bias = sb("down", [P, E1, C]), sb("down_bias", [E1, C])
        ident, identb = sb("ident", [P, P]), sb("identb", [P, P], BF16)
        mask_qk, mask_kq = sb("mask_qk", [P, P], BF16), sb("mask_kq", [P, P], BF16)
        expert0, expert1 = sb("expert0", [P, E0 * K0]), sb("expert1", [P, E1 * K1])
        pick = sb("pick", [NPART * 2 * NS, 2 * NS], BF16)
        minus_half = sb("minus_half", [P, NT])

        xin, xn, xnT = sb("xin", [P, NT, C]), sb("xn", [P, NT, C]), sb("xnT", [P, T])
        tmp = sb("tmp", [P, 4 * T])
        t1, t2, qf, kf = (tmp[:, i * T:(i + 1) * T] for i in range(4))
        parts = sb("parts", [P, 2, NPART, T], BF16)
        qs, ks = sb("qs", [P, H, T], BF16), sb("ks", [P, H, T], BF16)
        vaug = sb("vaug", [P, NT, H * (HD + 1) + STRIP - HD - 1])
        mx = sb("mx", [P, NT, H])
        mparts = parts[0:H, 0, 0:2, :]
        recip = sb("recip", [P, 2, H // 2])
        x1, xa = sb("x1", [P, NT, C]), sb("xa", [P, NT, C])
        st_a, mv_a = sb("st_a", [P, NT, 6]), sb("mv_a", [P, NT, 2])
        ve_a, rstd_a = sb("ve_a", [P, NT]), sb("rstd_a", [P, NT])

        x2 = sb("x2", [P, NT, C])
        nb = sb("nb", [P, NT, C])
        xl, ynT = sb("xl", [P, NT, C]), sb("ynT", [P, T])
        upad = sb("upad", [P, ND * NSEQ, NC - 1 + S])
        u = sb("u", [P, ND, T])
        dt = sb("dt", [P, ND, T])
        y = sb("y", [P, ND, 2, T])
        dtin = sb("dtin", [2 * NS + NDT, T])
        bcp = sb("bcp", [NPART * 2 * NS, T], BF16)
        bcr, bc2 = dtin[0:2 * NS, :], sb("bc2", [2 * NS, T], BF16)
        brow = sb("brow", [P, 2, T])
        da = sb("da", [P, 2, 2 * T])
        dbu = sb("dbu", [P, 2, 2 * T])
        hst = sb("hst", [P, 2, 2 * T])
        yhh, yhl = sb("yhh", [P, T], F32R), sb("yhl", [P, T], F32R)
        acc = sb("acc", [P, NT, C])
        st_b, mv_b = sb("st_b", [P, NT, 6]), sb("mv_b", [P, NT, 2])
        ve_b, rstd_b = sb("ve_b", [P, NT]), sb("rstd_b", [P, NT])
        zs = upad[:, :, NC - 1:NC - 1 + S]
        sp_x, sp_e = dbu[:, 0, :], dbu[:, 1, :]
        sp_w, sp_l = hst[:, 0, :], hst[:, 1, :]
        gate_b = [dbu[:, 0, 0:T], dbu[:, 0, T:2 * T]]
        tanh_b = [dbu[:, 1, 0:T], dbu[:, 1, T:2 * T]]
        up_b = [hst[:, 0, 0:T], hst[:, 0, T:2 * T]]
        weighed = [y[:, 0, 1, :], y[:, 1, 1, :]]
        act_bufs = [hst[:, 1, 0:T], hst[:, 1, T:2 * T]]

        def routing(name, e, k):
            return {"e": e, "k": k,
                    "ex": sb(name + "ex", [P, NT, e]), "m": sb(name + "m", [P, NT]),
                    "top": sb(name + "top", [P, NT, 8]), "idx": sb(name + "idx", [P, NT, 8], U32),
                    "idxf": sb(name + "idxf", [P, NT, 8]), "wk": sb(name + "wk", [P, NT, k]),
                    "r": sb(name + "r", [P, NT]), "hot": sb(name + "hot", [P, NT, e * k]),
                    "g": sb(name + "g", [P, NT, e])}

        ro0, ro1 = routing("ra_", E0, K0), routing("rb_", E1, K1)
        half_gates = sb("half_gates", [P, NT, E1])
        gT = dtin[0:E1, :]

        part_dram = nc.dram_tensor("part_scratch", (2, NPART, HD, H, T), BF16, kind="Internal").ap()
        max_dram = nc.dram_tensor("max_scratch", (2, H, T), BF16, kind="Internal").ap()

        ps_sc = ctx.enter_context(nc.psum_tensor("ps_sc", [P, 2, 2 * T], F32))
        ps_am = ctx.enter_context(nc.psum_tensor("ps_am", [P, T], F32))
        ps_bc = ctx.enter_context(nc.psum_tensor("ps_bc", [P, 2 * T], F32))
        ps_bb = ctx.enter_context(nc.psum_tensor("ps_bb", [P, T], F32))

        def ring(name, bufs, uses, quiet=(), kept=()):
            return Ring(bufs, [sem(f"{name}_full{b}") for b in range(len(bufs))],
                        [sem(f"{name}_free{b}") for b in range(len(bufs))], uses, quiet, kept)

        sc = ring("sc", [ps_sc[:, b, :] for b in range(2)],
                  attention_uses(0) + attention_uses(1))
        am = ring("am", [ps_am[:, :]],
                  [(n, a) for a in range(2) for n in
                   ["xT", "v"] + [("pv", s, half) for s in range(NSEQ) for half in range(2)] + ["oT", "proj"]],
                  quiet=[(("pv", s, half), a) for a in range(2) for s in range(NSEQ) for half in range(2)])
        bb = ring("bb", [ps_bb[:, :]],
                  ["xfT", "router0"] + [("down0", e) for e in range(E0)] + ["ynT", "dbc"] + [("B", n) for n in range(NS)]
                  + ["out", "yhT", "router1", "gT", "bias"] + [("down1", e) for e in range(E1)])
        bc = ring("bc", [ps_bc[:, :]],
                  [("up", e) for e in range(E0)] + ["u", "z", "dt"] + [("C", g) for g in range(NCH)] + [("gu", e) for e in range(E1)],
                  kept=[("C", g) for g in range(NCH)])
        PROBS = [("st", a, s, g) for a in range(2) for s in range(NSEQ) for g in range(H // 2)]
        pr = ring("pr", [tmp[:, b * 768:(b + 1) * 768] for b in range(2)],
                  PROBS, quiet=PROBS)
        hid_bufs = [dbu[:, b, :] for b in range(2)]
        chunks = [(g, d) for g in range(NCH) for d in range(ND)]
        dar = ring("dar", [da[:, b, :] for b in range(2)], chunks)
        dbr = ring("dbr", [dbu[:, b, :] for b in range(2)], chunks)
        hsr = ring("hsr", [hst[:, b, :] for b in range(2)], chunks)
        act_ready = signal("act_ready", E1)

        w_load = sem("w_load")
        w_ready = sem("w_ready")
        w_decay = sem("w_decay")
        x_loaded = signal("x_loaded", 16)
        var_a, rstd_s_a, norm_a = signal("var_a", 4), signal("rstd_s_a", 4), signal("norm_a", 4)
        var_b, rstd_s_b, norm_b = signal("var_b", 3), signal("rstd_s_b", 3), signal("norm_b", 3)
        qk_ready = signal("qk_ready", 2)
        p1_ready = signal("p1_ready", 4)
        rest_ready = signal("rest_ready", 2)
        p2_ready, p3_ready = signal("p2_ready", 4), signal("p3_ready", 4)
        parts_out = signal("parts_out", 2 * PART_DMAS * 16)
        stacked = signal("stacked", 2 * STACK_DMAS * 16)
        m1_ready = signal("m1_ready", 4)
        max_out = signal("max_out", 4 * 16)
        max_in = [signal(f"max_in{s}", 2 * 16) for s in range(NSEQ)]
        xbias_ready = signal("xbias_ready", 1)
        acc0_ready = signal("acc0_ready", 1)
        xf_ready, xfl_ready, logits_ready = signal("xf_ready", 1), signal("xfl_ready", 1), signal("logits_ready", 1)
        ex0_ready = signal("ex0_ready", 1)
        base_ready = signal("base_ready", 1)
        conv_ready, u_ready = signal("conv_ready", 1), signal("u_ready", 1)
        b1_ready, b2_ready, b2c_ready, b3_ready = (signal(n, 1) for n in ("b1_ready", "b2_ready", "b2c_ready", "b3_ready"))
        spe_ready, spw_ready, spl_ready = signal("spe_ready", 1), signal("spw_ready", 1), signal("spl_ready", 1)
        dt_ready, dtu_ready = signal("dt_ready", 1), signal("dtu_ready", 1)
        y_sum, y_skip, y_ready = signal("y_sum", 1), signal("y_skip", 1), signal("y_ready", 1)
        yhf_ready, yhl_ready = signal("yhf_ready", 1), signal("yhl_ready", 1)
        lg1_ready, ex1_ready, g1_ready = signal("lg1_ready", 1), signal("ex1_ready", 1), signal("g1_ready", 1)
        gate_ready, tanh_ready = signal("gate_ready", E1), signal("tanh_ready", E1)
        halved, acc_added = signal("halved", 1), signal("acc_added", E1)
        out_stored = signal("out_stored", 16)

        dve_a = Steps(sem("dve_a"), STEPS_DVE_A)
        dve_b = Steps(sem("dve_b"), STEPS_DVE_B)
        act_steps = Steps(sem("act_steps"), STEPS_ACT)

        raw_w1, raw_gu = da, (dbu, hst)
        W_RAW = [
            (raw_w1[:].rearrange("p a b -> p (a b)"), inp["w1"]),
            (raw_gu[0][:].rearrange("p a (e n) -> p (a e) n", n=2 * F1),
             inp["gate_up"][0:E1 // 2].rearrange("e h n -> h e n")),
            (raw_gu[1][:].rearrange("p a (e n) -> p (a e) n", n=2 * F1),
             inp["gate_up"][E1 // 2:E1].rearrange("e h n -> h e n")),
            (tmp[:, 0:P], inp["mask_qk"]), (tmp[:, P:2 * P], inp["mask_kq"]), (ident[:, :], inp["ident"]), (tmp[0:NPART * 2 * NS, 2 * P:2 * P + 2 * NS], inp["pick"]),
            (decay[:, :, :], inp["A_log"].rearrange("(d p) n -> p d n", p=P)),
        ]
        W_REST = [
            (ks[KS:KM, :, :], inp["ones"]),
            (wq[:, :], inp["wqT"]), (wqs[:, :], inp["wqsT"]), (wk[:, :], inp["wkT"]), (wks[:, :], inp["wksT"]),
            (wv[:, :], inp["wvT"]), (wo[:, :], inp["woT"]), (qk_bias[:, :], inp["qk_bias"]),
            (bv[:, :], inp["bv"]), (bo[:, :], inp["bo"]), (cos[:, :], inp["cos"]), (sin[:, :], inp["sin"]),
            (c_attn[:, :], inp["c_attn"]), (c_proj[:, :], inp["c_proj"]),
            (ln1[:, :], inp["ln1"]), (ln2[:, :], inp["ln2"]), (ln_g[:, :], inp["ln_g"]), (ln_b[:, :], inp["ln_b"]),
            (router0[:, :], inp["router0"]), (router1[:, :], inp["router1T"]),
            (w2[:, :, :], inp["w2"].rearrange("(k p) c -> p k c", p=P)),
            (win[:, :], inp["WinT"]),
            (conv_w[:, :, :], inp["conv_w"].rearrange("(d p) k -> p d k", p=P)),
            (conv_b[:, :], inp["conv_b"]),
            (wx[:, :, :], inp["WxT"].rearrange("(d p) r -> p d r", p=P)),
            (wdt[2 * NS:2 * NS + NDT, :], inp["WdtT"]),
            (dt_bias[:, :], inp["dt_bias"]),
            (skip[:, :], inp["D"]),
            (wout[:, :, :], inp["WoutT"].rearrange("(d p) c -> p d c", p=P)),
            (router_bias[:, :], inp["router_bias"]),
            (gu_bias[:, :], inp["gate_up_biasT"]),
            (down[:, :, :], inp["down"].rearrange("e f c -> f e c")),
            (down_bias[:, :], inp["down_bias"]),
            (expert0[:, :], inp["expert0"]), (expert1[:, :], inp["expert1"]),
        ]
        LOADS = 16 * (len(W_RAW) + len(W_REST))

        block = ctx.enter_context(nc.Block())

        @block.sync
        def _(sp):
            for dst, src in W_RAW + W_REST:
                sp.dma_start(dst, src).then_inc(w_load, 16)

            def counted(*marks):
                for _, value in marks:
                    sp.lower_val(value)
                return marks

            def front(it, load_next):
                split = counted(*(part.at(it, 2 * a + w + 1) for a in range(2)
                                  for part in (p1_ready, p2_ready, p3_ready) for w in range(2)))
                copied = counted(*(parts_out.at(it, 16 * PART_DMAS * (a + 1)) for a in range(2)))
                maxima = counted(*(sc.released(it, ("mT", a, s)) for a in range(2) for s in range(NSEQ)))
                max_copied = counted(*(max_out.at(it, 16 * (n + 1)) for n in range(2 * NSEQ)))
                xin_read = counted(norm_a.at(it, 1), xbias_ready.at(it, 1))
                for a in range(2):
                    for i in range(NPART):
                        for w in range(2):
                            sp.wait_ge(*split[(a * NPART + i) * 2 + w])
                            sp.dma_start(part_dram[w, i].rearrange("d h t -> h d t"), parts[:, w, i, :])\
                              .then_inc(parts_out.sem, 16)
                    sp.wait_ge(*copied[a])
                    for i in range(NPART):
                        rows = slice(i * NPART * HD, (i + 1) * NPART * HD)
                        q_part = part_dram[0, i].rearrange("d h t -> d (h t)")
                        sp.dma_start(qs[rows, :, :].rearrange("r h t -> r (h t)"),
                                     q_part.unsqueeze(0).to_broadcast([NPART, HD, H * T])).then_inc(stacked.sem, 16)
                        sp.dma_start(ks[rows, :, :], part_dram[1].rearrange("j d h t -> (j d) h t"))\
                          .then_inc(stacked.sem, 16)
                    if a == 0 and load_next:
                        for mark in xin_read:
                            sp.wait_ge(*mark)
                        sp.dma_start(xin[:, :, :], x_dram[it + 1]).then_inc(x_loaded.sem, 16)
                    for s in range(NSEQ):
                        cols = slice(s * S, (s + 1) * S)
                        sp.wait_ge(*maxima[NSEQ * a + s])
                        sp.dma_start(max_dram[:, :, cols].rearrange("i h t -> h i t"), mparts[:, :, cols])\
                          .then_inc(max_out.sem, 16)
                        sp.wait_ge(*max_copied[NSEQ * a + s])
                        sp.dma_start(qs[KS:KM, :, cols], max_dram[:, :, cols]).then_inc(max_in[s].sem, 16)

            def back(it):
                finished, = counted(acc_added.at(it, E1))
                sp.wait_ge(*finished)
                sp.dma_start(out_dram[it], acc[:, :, :]).then_inc(out_stored.sem, 16)

            sp.dma_start(xin[:, :, :], x_dram[0]).then_inc(x_loaded.sem, 16)
            front(0, True)
            front(1, True)
            back(0)
            with sp.Fori(1, pairs - 2) as it:
                front(it + 1, True)
                back(it)
            front(pairs - 1, False)
            back(pairs - 2)
            back(pairs - 1)
            sp.wait_ge(*out_stored.at(pairs, 0))

        @block.tensor
        def _(pe):
            mm, transpose = nc.tensor.matmul, nc.tensor.transpose

            def turn(src, dst):
                for t in range(NT):
                    last = transpose(dst[:, t * P:(t + 1) * P], src[:, t, :], ident[:, :])
                return last

            def x_turn(it, a):
                pe.wait_ge(*norm_a.at(it, 1 if a == 0 else 3))
                pe.wait_ge(*am.emptied(it, ("xT", a)))
                turn(xn, am.buf(("xT", a))).then_inc(am.sem_full(("xT", a)), 1)

            def qk(it, a):
                pe.wait_ge(*am.released(it, ("xT", a)))
                if a == 0:
                    for which, w, ws in (("q", wq, wqs), ("k", wk, wks)):
                        pe.wait_ge(*sc.emptied(it, (which, a)))
                        dst = sc.buf((which, a))
                        mm(dst[:, 0:T], w[:, :], xnT[:, :], start=True, stop=True)
                        mm(dst[:, T:2 * T], ws[:, :], xnT[:, :], start=True, stop=True)\
                            .then_inc(sc.sem_full((which, a)), 1)
                else:
                    for which, lo in (("q", 0), ("k", C)):
                        pe.wait_ge(*sc.emptied(it, (which, a)))
                        mm(sc.buf((which, a))[:, 0:T], c_attn[:, lo:lo + C], xnT[:, :], start=True, stop=True)\
                            .then_inc(sc.sem_full((which, a)), 1)

            def v(it, a):
                pe.wait_ge(*am.emptied(it, ("v", a)))
                for t in range(NT):
                    last = mm(am.buf(("v", a))[:, t * P:(t + 1) * P], xnT[:, t * P:(t + 1) * P],
                              wv[:, :] if a == 0 else c_attn[:, 2 * C:3 * C], start=True, stop=True)
                last.then_inc(am.sem_full(("v", a)), 1)

            def max_pass(it, a, s, g):
                use = ("max", a, s, g)
                dst = sc.buf(use)
                pe.wait_ge(*sc.emptied(it, use))
                if s == 0 and g == 0:
                    pe.wait_ge(*stacked.at(it, STACK_DMAS * 16 * (a + 1)))
                qt, heads, n = (1, range(4 * g, 4 * g + 4), S) if g < 4 else (0, range(8 * (g - 4), 8 * (g - 3)), P)
                for j, h in enumerate(heads):
                    q0 = s * S + qt * P
                    mm(dst[:, (j + 1) * n - P:(j + 1) * n], identb[:, :], mask_qk[:, :],
                       start=True, stop=False, skip_group_check=True)
                    last = mm(dst[:, j * n:(j + 1) * n], qs[0:KS, h, q0:q0 + P], ks[0:KS, h, s * S:s * S + n],
                              start=False, stop=True, skip_group_check=True)
                last.then_inc(sc.sem_full(use), 1)

            def max_turn(it, a, s):
                use = ("mT", a, s)
                pe.wait_ge(*sc.emptied(it, use))
                for g in (4, 5):
                    pe.wait_ge(*sc.released(it, ("max", a, s, g)))
                for t in range(2):
                    last = transpose(sc.buf(use)[0:H, t * P:(t + 1) * P], mx[:, 2 * s + t, :], ident[:, :])
                last.then_inc(sc.sem_full(use), 1)

            def scores(it, a, s, g):
                use = ("st", a, s, g)
                dst = sc.buf(use)
                pe.wait_ge(*sc.emptied(it, use))
                if g == 0:
                    pe.wait_ge(*max_in[s].at(it, 16 * (a + 1)))
                for j in range(2):
                    h, s0 = 2 * g + j, s * S
                    mm(dst[:, j * S:j * S + P], identb[:, :], mask_kq[:, :],
                       start=True, stop=False, skip_group_check=True)
                    mm(dst[:, j * S:(j + 1) * S], ks[0:KM, h, s0:s0 + P], qs[0:KM, h, s0:s0 + S],
                       start=False, stop=True, skip_group_check=True)
                for j in range(2):
                    h, s0 = 2 * g + j, s * S + P
                    cols = dst[:, 2 * S + j * P:2 * S + (j + 1) * P]
                    mm(cols, identb[:, :], mask_kq[:, :], start=True, stop=False)
                    last = mm(cols, ks[0:KM, h, s0:s0 + P], qs[0:KM, h, s0:s0 + P], start=False, stop=True)
                last.then_inc(sc.sem_full(use), 1)

            def values(it, a, s, g):
                use = ("st", a, s, g)
                half = g // (H // 4)
                bank = (("pv", s, half), a)
                if g % (H // 4) == 0:
                    pe.wait_ge(*am.emptied(it, bank))
                if s == 0 and g == 0:
                    pe.wait_ge(*am.released(it, ("v", a)))
                pe.wait_ge(*sc.released(it, use))
                prob = pr.buf(use)
                for j in range(2):
                    h = 2 * g + j
                    rows, col = slice(h % 4 * STRIP, (h % 4 + 1) * STRIP), h % 8 // 4 * S
                    cols_v = slice(h * (HD + 1), h * (HD + 1) + STRIP)
                    mm(am.buf(bank)[rows, col:col + S], vaug[:, 2 * s, cols_v], prob[:, j * S:(j + 1) * S],
                       start=True, stop=False, skip_group_check=True)
                    last = mm(am.buf(bank)[rows, col + P:col + S], vaug[:, 2 * s + 1, cols_v],
                              prob[:, 2 * S + j * P:2 * S + (j + 1) * P], start=False, stop=True, skip_group_check=True)
                last.then_inc(pr.sem_free(use), 1)

            def values_turn(it, a, s, half):
                use = ("vT", a, s, half)
                pe.wait_ge(*am.released(it, (("pv", s, half), a)))
                pe.wait_ge(*sc.emptied(it, use))
                for qt in range(2):
                    for four in range(2):
                        last = transpose(sc.buf(use)[:, (2 * qt + four) * P:(2 * qt + four + 1) * P],
                                         xnT[:, four * S + qt * P:four * S + (qt + 1) * P], ident[:, :])
                last.then_inc(sc.sem_full(use), 1)

            def out_turn(it, a):
                pe.wait_ge(*sc.released(it, ("vT", a, NSEQ - 1, 1)))
                pe.wait_ge(*am.emptied(it, ("oT", a)))
                turn(xn, am.buf(("oT", a))).then_inc(am.sem_full(("oT", a)), 1)

            def out_project(it, a):
                pe.wait_ge(*am.released(it, ("oT", a)))
                pe.wait_ge(*am.emptied(it, ("proj", a)))
                for t in range(NT):
                    last = mm(am.buf(("proj", a))[:, t * P:(t + 1) * P], xnT[:, t * P:(t + 1) * P],
                              (wo if a == 0 else c_proj)[:, :], start=True, stop=True)
                last.then_inc(am.sem_full(("proj", a)), 1)

            def attend(it, a, s, g):
                scores(it, a, s, g)
                if g >= 1:
                    values(it, a, s, g - 1)
                if g == H // 2 - 1:
                    values(it, a, s, g)
                if g == 5:
                    values_turn(it, a, s, 0)
                if g == 1 and s >= 1:
                    values_turn(it, a, s - 1, 1)

            def nb_turn(it, use, norm, k):
                pe.wait_ge(*norm.at(it, k + 1))
                pe.wait_ge(*bb.emptied(it, use))
                turn(nb, bb.buf(use)).then_inc(bb.sem_full(use), 1)

            def route(it, use, copied, router, e):
                pe.wait_ge(*copied.at(it, 1))
                pe.wait_ge(*bb.emptied(it, use))
                for t in range(NT):
                    last = mm(bb.buf(use)[:, t * e:(t + 1) * e], ynT[:, t * P:(t + 1) * P], router[:, :],
                              start=True, stop=True)
                last.then_inc(bb.sem_full(use), 1)

            def up(it, e):
                use = ("up", e)
                if e == 0:
                    pe.wait_ge(*xfl_ready.at(it, 1))
                pe.wait_ge(*bc.emptied(it, use))
                for f in range(2):
                    dst = bc.buf(use)[:, f * T:(f + 1) * T]
                    cols = slice((2 * e + f) * P, (2 * e + f + 1) * P)
                    mm(dst, w1h[:, cols], yhh[:, :], start=True, stop=False)
                    mm(dst, w1h[:, cols], yhl[:, :], start=False, stop=False)
                    last = mm(dst, w1l[:, cols], yhh[:, :], start=False, stop=True)
                last.then_inc(bc.sem_full(use), 1)

            def down0(it, e):
                use = ("down0", e)
                pe.wait_ge(*bc.released(it, ("up", e)))
                pe.wait_ge(*bb.emptied(it, use))
                hid = hid_bufs[e % 2]
                for t in range(NT):
                    for f in range(2):
                        last = mm(bb.buf(use)[:, t * P:(t + 1) * P],
                                  hid[:, f * T + t * P:f * T + (t + 1) * P], w2[:, 2 * e + f, :],
                                  start=(f == 0), stop=(f == 1))
                last.then_inc(bb.sem_full(use), 1)

            def project_in(it, use, lo):
                if use == "u":
                    pe.wait_ge(*bb.released(it, "ynT"))
                pe.wait_ge(*bc.emptied(it, use))
                for d in range(ND):
                    last = mm(bc.buf(use)[:, d * T:(d + 1) * T], win[:, lo + d * P:lo + (d + 1) * P], ynT[:, :],
                              start=True, stop=True)
                last.then_inc(bc.sem_full(use), 1)

            def project_x(it):
                pe.wait_ge(*u_ready.at(it, 1))
                pe.wait_ge(*bb.emptied(it, "dbc"))
                for d in range(ND):
                    last = mm(bb.buf("dbc")[0:2 * NS + NDT, :], wx[:, d, :], u[:, d, :], start=(d == 0), stop=(d == ND - 1))
                last.then_inc(bb.sem_full("dbc"), 1)

            def project_dt(it):
                pe.wait_ge(*b1_ready.at(it, 1))
                pe.wait_ge(*bc.emptied(it, "dt"))
                for d in range(ND):
                    last = mm(bc.buf("dt")[:, d * T:(d + 1) * T], wdt[2 * NS:2 * NS + NDT, d * P:(d + 1) * P],
                              dtin[2 * NS:2 * NS + NDT, :], start=True, stop=True)
                last.then_inc(bc.sem_full("dt"), 1)

            def spread(dst, row):
                return mm(dst, pick[:, row:row + 1].to_broadcast([NPART * 2 * NS, P]), bcp[:, :],
                          start=True, stop=True)

            def spread_b(it, g):
                if g == 0:
                    pe.wait_ge(*b2c_ready.at(it, 1))
                    pe.wait_ge(*b3_ready.at(it, 1))
                for j in range(2):
                    n = 2 * g + j
                    pe.wait_ge(*bb.emptied(it, ("B", n)))
                    spread(bb.buf(("B", n)), n).then_inc(bb.sem_full(("B", n)), 1)

            def spread_c(it, g):
                pe.wait_ge(*bc.emptied(it, ("C", g)))
                if g >= 1:
                    pe.wait_ge(*hsr.filled(it, (g - 1, ND - 1)))
                for j in range(2):
                    last = spread(bc.buf(("C", g))[:, j * T:(j + 1) * T], NS + 2 * g + j)
                last.then_inc(bc.sem_full(("C", g)), 1)

            def project_out(it):
                pe.wait_ge(*y_ready.at(it, 1))
                pe.wait_ge(*bb.emptied(it, "out"))
                for t in range(NT):
                    for d in range(ND):
                        last = mm(bb.buf("out")[:, t * P:(t + 1) * P], y[:, d, 0, t * P:(t + 1) * P], wout[:, d, :],
                                  start=(d == 0), stop=(d == ND - 1))
                last.then_inc(bb.sem_full("out"), 1)

            def gate_up(it, e):
                use = ("gu", e)
                if e == 0:
                    pe.wait_ge(*yhl_ready.at(it, 1))
                pe.wait_ge(*bc.emptied(it, use))
                for f in range(2):
                    dst = bc.buf(use)[:, f * T:(f + 1) * T]
                    cols = slice(f * F1, (f + 1) * F1)
                    mm(dst, guh[:, e, cols], yhh[:, :], start=True, stop=False)
                    mm(dst, guh[:, e, cols], yhl[:, :], start=False, stop=False)
                    last = mm(dst, gul[:, e, cols], yhh[:, :], start=False, stop=True)
                last.then_inc(bc.sem_full(use), 1)

            def gate_bias(it):
                pe.wait_ge(*g1_ready.at(it, 1))
                pe.wait_ge(*bb.emptied(it, "gT"))
                for t in range(NT):
                    last = transpose(bb.buf("gT")[0:E1, t * P:(t + 1) * P], ro1["g"][:, t, :], ident[:, :])
                last.then_inc(bb.sem_full("gT"), 1)
                pe.wait_ge(*bb.released(it, "gT"))
                pe.wait_ge(*bb.emptied(it, "bias"))
                for t in range(NT):
                    last = mm(bb.buf("bias")[:, t * P:(t + 1) * P], gT[:, t * P:(t + 1) * P], down_bias[:, :],
                              start=True, stop=True)
                last.then_inc(bb.sem_full("bias"), 1)

            def down1(it, e):
                use = ("down1", e)
                pe.wait_ge(*act_ready.at(it, e + 1))
                pe.wait_ge(*bb.emptied(it, use))
                for t in range(NT):
                    last = mm(bb.buf(use)[:, t * P:(t + 1) * P], act_bufs[e % 2][:, t * P:(t + 1) * P],
                              down[:, e, :], start=True, stop=True)
                last.then_inc(bb.sem_full(use), 1)

            def together(a, b):
                front, back = steps_of(a, b)
                back(nb_turn, "xfT", norm_a, 3)
                back(route, "router0", xf_ready, router0, E0)
                back(up, 0)
                front(x_turn, 0)
                front(qk, 0)
                for e in range(E0):
                    if e + 1 < E0:
                        back(up, e + 1)
                    back(down0, e)
                    if e == 0:
                        front(v, 0)
                    if e >= E0 - 2:
                        front(max_pass, 0, 0, e - (E0 - 2))
                for g in (2, 3, 4, 5):
                    front(max_pass, 0, 0, g)
                back(nb_turn, "ynT", norm_b, 1)
                front(max_pass, 0, 1, 0)
                back(project_in, "u", 0)
                back(project_in, "z", DIN)
                front(max_pass, 0, 1, 1)
                front(max_turn, 0, 0)
                back(project_x)
                for g in (2, 3):
                    front(max_pass, 0, 1, g)
                back(project_dt)
                for g in (4, 5):
                    front(max_pass, 0, 1, g)
                back(spread_b, 0)
                front(max_turn, 0, 1)
                front(attend, 0, 0, 0)
                back(spread_c, 0)
                for g in range(1, 6):
                    front(attend, 0, 0, g)
                for c, (g, d) in enumerate(chunks):
                    if d == 0 and g >= 1:
                        back(spread_c, g)
                    if d == 0 and g + 1 < NCH:
                        back(spread_b, g + 1)
                    for n in SCORES_AT[c]:
                        front(attend, 0, n // (H // 2), n % (H // 2))
                    if c == OUT_AT - 1:
                        front(values_turn, 0, NSEQ - 1, 1)
                    if c == OUT_AT:
                        front(out_turn, 0)
                    if c == OUT_AT + 1:
                        front(out_project, 0)
                    if c == NEXT_AT:
                        front(x_turn, 1)
                        front(qk, 1)
                        front(v, 1)
                for g in range(4):
                    front(max_pass, 1, 0, g)
                back(project_out)
                front(max_pass, 1, 0, 4)
                back(nb_turn, "yhT", norm_b, 2)
                front(max_pass, 1, 0, 5)
                back(route, "router1", yhf_ready, router1, E1)
                for g in range(2):
                    front(max_pass, 1, 1, g)
                back(gate_up, 0)
                front(max_turn, 1, 0)
                for g in (2, 3):
                    front(max_pass, 1, 1, g)
                back(gate_bias)
                for g in (4, 5):
                    front(max_pass, 1, 1, g)
                front(max_turn, 1, 1)
                back(gate_up, 1)
                for g in range(2):
                    front(attend, 1, 0, g)
                for e in range(E1):
                    if 1 <= e < E1 - 1:
                        back(gate_up, e + 1)
                    for n in ATTEND_AT[e]:
                        front(attend, 1, n // (H // 2), n % (H // 2))
                    back(down1, e)
                    if e == OUT1_AT - 1:
                        front(values_turn, 1, NSEQ - 1, 1)
                    if e == OUT1_AT:
                        front(out_turn, 1)
                    if e == OUT1_AT + 1:
                        front(out_project, 1)

            pe.wait_ge(w_load, LOADS)
            pe.wait_ge(w_ready, W_READY)
            together(0, None)
            together(1, 0)
            with pe.Fori(1, pairs - 1) as it:
                together(it + 1, it)
            together(None, pairs - 1)

        @block.vector
        def _(dve):
            V = nc.vector

            def statistics(it, k, steps, src, stats, mv, ve, var):
                for t in range(NT):
                    last = V.bn_stats(stats[:, t, :], src[:, t, :])
                steps.note(last)
                dve.wait_ge(*steps.now(it))
                V.memset(ve[:, :], 0.0)
                for t in range(NT):
                    last = V.bn_aggr(mv[:, t, :], stats[:, t, :])
                steps.note(last)
                dve.wait_ge(*steps.now(it))
                V.tensor_scalar(ve[:, :], mv[:, :, 1], EPS, None, ALU.add).then_inc(var.sem, 1)

            def apply(it, k, src, dst, mv, rstd, rstd_s, norm):
                dve.wait_ge(*rstd_s.at(it, k + 1))
                for t in range(NT):
                    last = V.tensor_scalar(dst[:, t, :], src[:, t, :], mv[:, t, 0:1], rstd[:, t:t + 1],
                                           ALU.subtract, ALU.mult)
                last.then_inc(norm.sem, 1)

            def stats_a(it, k, src):
                statistics(it, k, dve_a, src, st_a, mv_a, ve_a, var_a)

            def apply_a(it, k, src, dst):
                apply(it, k, src, dst, mv_a, rstd_a, rstd_s_a, norm_a)

            def stats_b(it, k, src):
                statistics(it, k, dve_b, src, st_b, mv_b, ve_b, var_b)

            def apply_b(it, k, src, dst):
                apply(it, k, src, dst, mv_b, rstd_b, rstd_s_b, norm_b)

            def rope(it):
                for k, (which, dst) in enumerate((("q", qf), ("k", kf))):
                    use = (which, 0)
                    dve.wait_ge(*sc.filled(it, use))
                    if k == 1:
                        dve.wait_ge(*qk_ready.at(it, 1))
                    for lo, col, table, to in ((0, 2 * k, cos, t1), (T, 2 * k + 1, sin, t2)):
                        last = V.scalar_tensor_tensor(
                            out=to.rearrange("p (s t) -> p s t", s=NSEQ),
                            in0=sc.buf(use)[:, lo:lo + T].rearrange("p (s t) -> p s t", s=NSEQ),
                            scalar=qk_bias[:, col:col + 1],
                            in1=table[:, :].unsqueeze(1).to_broadcast([P, NSEQ, S]),
                            op0=ALU.add, op1=ALU.mult)
                    last.then_inc(sc.sem_free(use), 1)
                    dve.wait_ge(*sc.released(it, use))
                    V.tensor_tensor(dst, t1, t2, ALU.add).then_inc(qk_ready.sem, 1)

            def rests(it, a):
                for k, (which, dst) in enumerate((("q", qf), ("k", kf))):
                    dve.wait_ge(*p1_ready.at(it, 2 * a + k + 1))
                    if a == 0:
                        V.tensor_tensor(dst, dst, parts[:, k, 0, :], ALU.subtract).then_inc(rest_ready.sem, 1)
                    else:
                        V.tensor_tensor(dst, sc.buf((which, 1))[:, 0:T], parts[:, k, 0, :], ALU.subtract)\
                            .then_inc(sc.sem_free((which, 1)), 1)

            def take_values(it, a):
                use = ("v", a)
                dve.wait_ge(*am.filled(it, use))
                for t in range(NT):
                    v = am.buf(use)[:, t * P:(t + 1) * P].rearrange("p (h d) -> p h d", d=HD)
                    to = vaug[:, t, 0:H * (HD + 1)].rearrange("p (h d) -> p h d", d=HD + 1)[:, :, 0:HD]
                    if a == 0:
                        last = V.tensor_tensor(to, v,
                                               bv[:, :].rearrange("p (h d) -> p h d", d=HD), ALU.add)
                    else:
                        last = V.tensor_copy(to, v)
                last.then_inc(am.sem_free(use), 1)

            def maximum(it, a, s, g):
                use = ("max", a, s, g)
                dve.wait_ge(*sc.filled(it, use))
                qt, h0, n = (1, 4 * g, S) if g < 4 else (0, 8 * (g - 4), P)
                V.tensor_reduce(mx[:, 2 * s + qt, h0:h0 + 2 * T // n], sc.buf(use).rearrange("p (h k) -> p h k", k=n),
                                AX.X, ALU.max, negate=True).then_inc(sc.sem_free(use), 1)

            def second_part(it, a, s):
                use = ("mT", a, s)
                dve.wait_ge(*sc.filled(it, use))
                dve.wait_ge(*m1_ready.at(it, NSEQ * a + s + 1))
                cols = slice(s * S, (s + 1) * S)
                V.tensor_tensor(mparts[:, 1, cols], sc.buf(use)[0:H, 0:S], mparts[:, 0, cols], ALU.subtract)\
                    .then_inc(sc.sem_free(use), 1)

            def normalise(it, a, s, half):
                use = ("vT", a, s, half)
                dve.wait_ge(*sc.filled(it, use))
                pv = sc.buf(use)[:, 0:4 * P].rearrange("p (t h d) -> p t h d", t=2, d=STRIP)
                dve_a.note(V.reciprocal(recip[:, :, :], pv[:, :, :, HD]))
                dve.wait_ge(*dve_a.now(it))
                cols = slice(half * C // 2, (half + 1) * C // 2)
                V.tensor_tensor(xn[:, 2 * s:2 * s + 2, cols].rearrange("p t (h d) -> p t h d", d=HD), pv[:, :, :, 0:HD],
                                recip[:, :, :].unsqueeze(3).to_broadcast([P, 2, H // 2, HD]), ALU.mult)\
                    .then_inc(sc.sem_free(use), 1)

            def residual(it, dst, use, other):
                dve.wait_ge(*am.filled(it, use))
                V.tensor_tensor(dst[:, :, :], am.buf(use).rearrange("p (t c) -> p t c", c=C), other[:, :, :], ALU.add)\
                    .then_inc(am.sem_free(use), 1)
                dve.wait_ge(*am.released(it, use))

            def route(it, steps, ro, exp_ready, sums_all, done=None):
                e, k = ro["e"], ro["k"]
                dve.wait_ge(*exp_ready.at(it, 1))
                if sums_all:
                    V.tensor_reduce(ro["r"][:, :], ro["ex"][:, :, :], AX.X, ALU.add)
                else:
                    V.memset(ro["r"][:, :], 0.0)
                for t in range(NT):
                    last = V.max(ro["top"][:, t, :], ro["ex"][:, t, :])
                steps.note(last)
                dve.wait_ge(*steps.now(it))
                if sums_all:
                    V.reciprocal(ro["m"][:, :], ro["r"][:, :])
                else:
                    V.tensor_reduce(ro["r"][:, :], ro["top"][:, :, 0:k], AX.X, ALU.add)
                for t in range(NT):
                    last = V.max_index(ro["idx"][:, t, :], ro["top"][:, t, :], ro["ex"][:, t, :])
                steps.note(last)
                dve.wait_ge(*steps.now(it))
                if not sums_all:
                    V.reciprocal(ro["m"][:, :], ro["r"][:, :])
                steps.note(V.tensor_copy(ro["idxf"][:, :, :], ro["idx"][:, :, :]))
                dve.wait_ge(*steps.now(it))
                V.tensor_tensor(ro["wk"][:, :, :], ro["top"][:, :, 0:k],
                                ro["m"][:, :].unsqueeze(2).to_broadcast([P, NT, k]), ALU.mult)
                names = (expert0 if ro is ro0 else expert1)[:, :].rearrange("p (e k) -> p e k", k=k)
                for t in range(NT):
                    last = V.tensor_tensor(ro["hot"][:, t, :].rearrange("p (e k) -> p e k", k=k), names,
                                           ro["idxf"][:, t, 0:k].unsqueeze(1).to_broadcast([P, e, k]), ALU.is_equal)
                steps.note(last)
                dve.wait_ge(*steps.now(it))
                for t in range(NT):
                    last = V.tensor_tensor(ro["hot"][:, t, :].rearrange("p (e k) -> p e k", k=k),
                                           ro["hot"][:, t, :].rearrange("p (e k) -> p e k", k=k),
                                           ro["wk"][:, t, :].unsqueeze(1).to_broadcast([P, e, k]), ALU.mult)
                steps.note(last)
                dve.wait_ge(*steps.now(it))
                last = V.tensor_reduce(ro["g"][:, :, :].rearrange("p t e -> p (t e)"),
                                       ro["hot"][:, :, :].rearrange("p t (e k) -> p (t e) k", k=k), AX.X, ALU.add)
                if done is None:
                    steps.note(last)
                    dve.wait_ge(*steps.now(it))
                else:
                    last.then_inc(done.sem, 1)
                    dve.wait_ge(*done.at(it, 1))

            def weigh(it, line, use, gates, e, total):
                dve.wait_ge(*line.filled(it, use))
                for t in range(NT):
                    last = V.scalar_tensor_tensor(out=total[:, t, :], in0=line.buf(use)[:, t * P:(t + 1) * P],
                                                  scalar=gates[:, t, e:e + 1], in1=total[:, t, :],
                                                  op0=ALU.mult, op1=ALU.add)
                last.then_inc(line.sem_free(use), 1)

            def split_x(it, use, ready):
                dve.wait_ge(*bb.released(it, use))
                V.tensor_tensor(yhl[:, :], ynT[:, :], yhh[:, :], ALU.subtract).then_inc(ready.sem, 1)

            def logits0(it):
                dve.wait_ge(*bb.filled(it, "router0"))
                logits = bb.buf("router0")[:, 0:NT * E0].rearrange("p (t e) -> p t e", e=E0)
                dve_b.note(V.tensor_reduce(ro0["m"][:, :], logits, AX.X, ALU.max))
                dve.wait_ge(*dve_b.now(it))
                V.tensor_tensor(ro0["ex"][:, :, :], logits, ro0["m"][:, :].unsqueeze(2).to_broadcast([P, NT, E0]),
                                ALU.subtract).then_inc(bb.sem_free("router0"), 1)

            def route0(it):
                route(it, dve_b, ro0, ex0_ready, False)
                dve.wait_ge(*acc0_ready.at(it, 1))

            def add0(it, e):
                if e >= 1:
                    dve.wait_ge(*bb.released(it, ("down0", e - 1)))
                weigh(it, bb, ("down0", e), ro0["g"], e, x2)

            def convolve(it):
                dve.wait_ge(*bc.released(it, "u"))
                for k in range(NC):
                    for d in range(ND):
                        src = upad[:, d * NSEQ:(d + 1) * NSEQ, k:k + S]
                        dst = u[:, d, :].rearrange("p (s t) -> p s t", s=NSEQ)
                        w = conv_w[:, d, k:k + 1]
                        if k == 0:
                            last = V.tensor_scalar(dst, src, w, conv_b[:, d:d + 1], ALU.mult, ALU.add)
                        else:
                            last = V.scalar_tensor_tensor(out=dst, in0=src, scalar=w, in1=dst,
                                                          op0=ALU.mult, op1=ALU.add)
                    if k < NC - 1:
                        dve_b.note(last)
                        dve.wait_ge(*dve_b.now(it))
                last.then_inc(conv_ready.sem, 1)

            def split_bc(it):
                dve.wait_ge(*b1_ready.at(it, 1))
                V.tensor_tensor(bcr[:, :], bb.buf("dbc")[0:2 * NS, :], bcp[0:2 * NS, :], ALU.subtract)\
                    .then_inc(bb.sem_free("dbc"), 1)
                dve.wait_ge(*b2_ready.at(it, 1))
                V.tensor_tensor(bcp[4 * NS:6 * NS, :], bcr[:, :], bc2[:, :], ALU.subtract).then_inc(b3_ready.sem, 1)

            def start_y(it):
                dve.wait_ge(*u_ready.at(it, 1))
                for d in range(ND):
                    last = V.tensor_scalar(y[:, d, 0, :], u[:, d, :], skip[:, d:d + 1], None, ALU.mult)
                last.then_inc(y_skip.sem, 1)

            def softplus_w(it):
                dve.wait_ge(*spe_ready.at(it, 1))
                V.tensor_scalar(sp_w, sp_e, 1.0, None, ALU.add).then_inc(spw_ready.sem, 1)

            def softplus(it):
                dve.wait_ge(*spw_ready.at(it, 1))
                dve_b.note(V.scalar_tensor_tensor(out=sp_e, in0=sp_w, scalar=-1.0, in1=sp_e,
                                                  op0=ALU.add, op1=ALU.subtract))
                dve.wait_ge(*dve_b.now(it))
                dve_b.note(V.scalar_tensor_tensor(out=sp_x, in0=sp_x, scalar=0.0, in1=sp_e,
                                                  op0=ALU.max, op1=ALU.subtract))
                dve.wait_ge(*dve_b.now(it))
                dve.wait_ge(*spl_ready.at(it, 1))
                V.tensor_tensor(dt[:, :, :].rearrange("p d t -> p (d t)"), sp_x, sp_l, ALU.add)\
                    .then_inc(dt_ready.sem, 1)

            def scan(it, c):
                use = chunks[c]
                dve.wait_ge(*dar.filled(it, use))
                dve.wait_ge(*dbr.filled(it, use))
                dve.wait_ge(*hsr.emptied(it, use))
                V.tensor_tensor_scan(hsr.buf(use), dar.buf(use), dbr.buf(use), 0.0, ALU.mult, ALU.add)\
                    .then_inc(dar.sem_free(use), 1)

            def times_c(it, c):
                use = chunks[c]
                g, d = use
                dve.wait_ge(*dar.released(it, use))
                if d == 0:
                    dve.wait_ge(*bc.filled(it, ("C", g)))
                V.tensor_tensor(hsr.buf(use), hsr.buf(use), bc.buf(("C", g)), ALU.mult)\
                    .then_inc(hsr.sem_full(use), 1)

            def dt_u(it):
                dve.wait_ge(*dt_ready.at(it, 1))
                dve.wait_ge(*y_skip.at(it, 1))
                V.tensor_tensor(u[:, :, :], dt[:, :, :], u[:, :, :], ALU.mult).then_inc(dtu_ready.sem, 1)

            def dt_b_u(it, c):
                use = chunks[c]
                dve.wait_ge(*dtu_ready.at(it, 1))
                dve.wait_ge(*bb.released(it, ("B", 2 * use[0] + 1)))
                if c >= 2:
                    dve.wait_ge(*dar.released(it, chunks[c - 2]))
                V.tensor_tensor(dbr.buf(use).rearrange("p (j t) -> p j t", j=2), brow[:, :, :],
                                u[:, use[1], :].unsqueeze(1).to_broadcast([P, 2, T]), ALU.mult)\
                    .then_inc(dbr.sem_full(use), 1)

            def finish_y(it):
                dve.wait_ge(*hsr.released(it, chunks[-1]))
                dve.wait_ge(*hsr.released(it, chunks[-2]))
                V.tensor_tensor(y[:, :, 0, :], y[:, :, 0, :], y[:, :, 1, :], ALU.add).then_inc(y_sum.sem, 1)
                dve.wait_ge(*y_sum.at(it, 1))
                dve.wait_ge(*bc.released(it, "z"))
                ys = y[:, :, 0, :].rearrange("p d (s t) -> p d s t", s=NSEQ)
                V.tensor_tensor(ys, ys, zs.rearrange("p (d s) t -> p d s t", s=NSEQ), ALU.mult).then_inc(y_ready.sem, 1)

            def add_out(it):
                dve.wait_ge(*bb.filled(it, "out"))
                dve.wait_ge(*base_ready.at(it, 1))
                V.tensor_tensor(xl[:, :, :], bb.buf("out").rearrange("p (t c) -> p t c", c=C), xl[:, :, :], ALU.add)\
                    .then_inc(bb.sem_free("out"), 1)
                dve.wait_ge(*bb.released(it, "out"))

            def logits1(it):
                dve.wait_ge(*bb.filled(it, "router1"))
                V.tensor_tensor(ro1["ex"][:, :, :], bb.buf("router1")[:, 0:NT * E1].rearrange("p (t e) -> p t e", e=E1),
                                router_bias[:, :].unsqueeze(1).to_broadcast([P, NT, E1]), ALU.add)\
                    .then_inc(bb.sem_free("router1"), 1)
                dve.wait_ge(*bb.released(it, "router1"))
                dve_b.note(V.tensor_reduce(ro1["m"][:, :], ro1["ex"][:, :, :], AX.X, ALU.max))
                dve.wait_ge(*dve_b.now(it))
                V.tensor_tensor(ro1["ex"][:, :, :], ro1["ex"][:, :, :],
                                ro1["m"][:, :].unsqueeze(2).to_broadcast([P, NT, E1]), ALU.subtract)\
                    .then_inc(lg1_ready.sem, 1)

            def route1(it):
                route(it, dve_b, ro1, ex1_ready, True, g1_ready)
                V.tensor_scalar(half_gates[:, :, :], ro1["g"][:, :, :], 0.5, None, ALU.mult).then_inc(halved.sem, 1)

            def start_acc(it):
                dve.wait_ge(*bb.filled(it, "bias"))
                dve.wait_ge(*out_stored.at(it, 0))
                V.tensor_tensor(acc[:, :, :], bb.buf("bias").rearrange("p (t c) -> p t c", c=C), xl[:, :, :], ALU.add)\
                    .then_inc(bb.sem_free("bias"), 1)
                dve.wait_ge(*bb.released(it, "bias"))

            def load_gate_up(it, e):
                use, b = ("gu", e), e % 2
                dve.wait_ge(*bc.filled(it, use))
                V.tensor_scalar(gate_b[b], bc.buf(use)[:, 0:T], gu_bias[:, e:e + 1], LIMIT, ALU.add, ALU.min)\
                    .then_inc(gate_ready.sem, 1)
                V.tensor_scalar(up_b[b], bc.buf(use)[:, T:2 * T], gu_bias[:, E1 + e:E1 + e + 1], LIMIT + 1,
                                ALU.add, ALU.min).then_inc(bc.sem_free(use), 1)

            def activate(it, e):
                b = e % 2
                dve.wait_ge(*bc.released(it, ("gu", e)))
                dve_b.note(V.scalar_tensor_tensor(out=up_b[b], in0=up_b[b], scalar=1.0 - LIMIT, in1=gate_b[b],
                                                  op0=ALU.max, op1=ALU.mult))
                dve.wait_ge(*dve_b.now(it))
                dve.wait_ge(*tanh_ready.at(it, e + 1))
                if e >= 2:
                    dve.wait_ge(*bb.filled(it, ("down1", e - 2)))
                V.scalar_tensor_tensor(out=act_bufs[b], in0=tanh_b[b], scalar=1.0, in1=up_b[b],
                                       op0=ALU.add, op1=ALU.mult).then_inc(act_ready.sem, 1)

            dve.wait_ge(w_load, LOADS)
            raw0, raw1, raw2 = (r[:].rearrange("p a n -> p (a n)") for r in (da, dbu, hst))
            guh_f, gul_f = (g[:].rearrange("p e n -> p (e n)") for g in (guh, gul))
            half = E1 * F1
            splits = ((w1h[:, :], w1l[:, :], raw0), (guh_f[:, 0:half], gul_f[:, 0:half], raw1),
                      (guh_f[:, half:], gul_f[:, half:], raw2))
            for hi, _, raw in splits:
                V.tensor_copy(hi, raw).then_inc(w_ready, 1)
            V.tensor_copy(mask_qk[:, :], tmp[:, 0:P]).then_inc(w_ready, 1)
            V.tensor_copy(mask_kq[:, :], tmp[:, P:2 * P]).then_inc(w_ready, 1)
            V.tensor_copy(identb[:, :], ident[:, :]).then_inc(w_ready, 1)
            V.tensor_copy(pick[:, :], tmp[0:NPART * 2 * NS, 2 * P:2 * P + 2 * NS]).then_inc(w_ready, 1)
            V.memset(vaug[:, :, :], 1.0).then_inc(w_ready, 1)
            V.memset(upad[:, :, 0:NC - 1], 0.0).then_inc(w_ready, 1)
            V.memset(minus_half[:, :], -0.5).then_inc(w_ready, 1)
            V.tensor_scalar(gu_bias[:, E1:2 * E1], gu_bias[:, E1:2 * E1], 1.0, None, ALU.add).then_inc(w_ready, 1)
            dve.wait_ge(w_ready, 3)
            for hi, lo, raw in splits:
                V.tensor_tensor(lo, raw, hi, ALU.subtract).then_inc(w_ready, 1)
            dve.wait_ge(w_ready, W_READY - 1)
            V.memset(da[:, :, :].rearrange("p b (j s) -> p (b j) s", s=S)[:, :, 0], 0.0).then_inc(w_ready, 1)

            def together(a, b):
                front, back = steps_of(a, b)
                dve_a.begin()
                dve_b.begin()
                if a is not None:
                    dve.wait_ge(*x_loaded.at(a, 16))
                front(stats_a, 0, xin)
                front(apply_a, 0, xin, xn)
                back(split_x, "xfT", xfl_ready)
                back(logits0)
                back(route0)
                front(rope)
                front(rests, 0)
                for e in range(E0):
                    back(add0, e)
                    if e == 0:
                        front(take_values, 0)
                    if e >= E0 - 2:
                        front(maximum, 0, 0, e - (E0 - 2))
                if b is not None:
                    dve.wait_ge(*bb.released(b, ("down0", E0 - 1)))
                back(stats_b, 0, x2)
                front(maximum, 0, 0, 2)
                back(apply_b, 0, x2, xl)
                if b is not None:
                    dve.wait_ge(*norm_b.at(b, 1))
                back(stats_b, 1, xl)
                front(maximum, 0, 0, 3)
                back(apply_b, 1, xl, nb)
                front(maximum, 0, 0, 4)
                front(maximum, 0, 0, 5)
                front(maximum, 0, 1, 0)
                back(convolve)
                front(maximum, 0, 1, 1)
                front(second_part, 0, 0)
                front(maximum, 0, 1, 2)
                front(maximum, 0, 1, 3)
                back(split_bc)
                back(start_y)
                front(maximum, 0, 1, 4)
                front(maximum, 0, 1, 5)
                back(softplus_w)
                front(second_part, 0, 1)
                back(softplus)
                back(dt_u)
                for c in range(len(chunks)):
                    if c + 1 in DVE_CHUNKS:
                        back(dt_b_u, c + 1)
                    back(scan, c)
                    back(times_c, c)
                    for s, half in normalised(SCORES_AT[c - 1] if c else [5]):
                        front(normalise, 0, s, half)
                    if c == OUT_AT:
                        front(normalise, 0, NSEQ - 1, 1)
                    if c == OUT_AT + 1:
                        if a is not None:
                            dve.wait_ge(*xbias_ready.at(a, 1))
                        front(residual, x1, ("proj", 0), x1)
                        front(stats_a, 1, x1)
                    if c == OUT_AT + 2:
                        front(apply_a, 1, x1, xa)
                        if a is not None:
                            dve.wait_ge(*norm_a.at(a, 2))
                        front(stats_a, 2, xa)
                    if c == OUT_AT + 3:
                        front(apply_a, 2, xa, xn)
                    if c == NEXT_AT:
                        front(rests, 1)
                        front(take_values, 1)
                for g in range(2):
                    front(maximum, 1, 0, g)
                back(finish_y)
                for g in (2, 3):
                    front(maximum, 1, 0, g)
                back(add_out)
                back(stats_b, 2, xl)
                front(maximum, 1, 0, 4)
                back(apply_b, 2, xl, nb)
                front(maximum, 1, 0, 5)
                back(split_x, "yhT", yhl_ready)
                back(logits1)
                for g in range(2):
                    front(maximum, 1, 1, g)
                back(load_gate_up, 0)
                front(second_part, 1, 0)
                back(route1)
                for g in (2, 3):
                    front(maximum, 1, 1, g)
                back(start_acc)
                for g in (4, 5):
                    front(maximum, 1, 1, g)
                front(second_part, 1, 1)
                for e in range(E1):
                    if e >= 1:
                        back(load_gate_up, e)
                    for s, half in normalised(ATTEND_AT[e - 1] if e else ()):
                        front(normalise, 1, s, half)
                    if e == OUT1_AT:
                        front(normalise, 1, NSEQ - 1, 1)
                    back(activate, e)
                    if e == OUT1_AT + 1:
                        front(residual, xa, ("proj", 1), xa)
                        front(stats_a, 3, xa)
                    if e == OUT1_AT + 2:
                        front(apply_a, 3, xa, nb)
                if a is not None:
                    dve_a.end()
                if b is not None:
                    dve_b.end()

            together(0, None)
            together(1, 0)
            with dve.Fori(1, pairs - 1) as it:
                together(it + 1, it)
            together(None, pairs - 1)

        @block.scalar
        def _(act):
            A = nc.scalar.activation

            def x_copy(it, a):
                use = ("xT", a)
                act.wait_ge(*am.filled(it, use))
                A(xnT[:, :], am.buf(use), ACT.Identity, scale=1.0 if a == 0 else ln1[:, 0:1])\
                    .then_inc(am.sem_free(use), 1)

            def first_parts(it, a):
                act.wait_ge(*parts_out.at(it, 16 * PART_DMAS * a))
                for k, (which, src) in enumerate((("q", qf), ("k", kf))):
                    if a == 0:
                        act.wait_ge(*qk_ready.at(it, k + 1))
                    else:
                        act.wait_ge(*sc.filled(it, (which, 1)))
                        src = sc.buf((which, 1))[:, 0:T]
                    A(parts[:, k, 0, :], src, ACT.Copy).then_inc(p1_ready.sem, 1)

            def second_parts(it, a):
                for k, (which, src) in enumerate((("q", qf), ("k", kf))):
                    if a == 0:
                        act.wait_ge(*rest_ready.at(it, k + 1))
                    else:
                        act.wait_ge(*sc.released(it, (which, 1)))
                    A(parts[:, k, 1, :], src, ACT.Copy).then_inc(p2_ready.sem, 1)

            def first_part(it, a, s):
                use = ("mT", a, s)
                act.wait_ge(*sc.filled(it, use))
                A(mparts[:, 0, s * S:(s + 1) * S], sc.buf(use)[0:H, 0:S], ACT.Copy).then_inc(m1_ready.sem, 1)

            def exponent(it, a, s, g):
                use = ("st", a, s, g)
                act.wait_ge(*sc.filled(it, use))
                act.wait_ge(*pr.emptied(it, use))
                A(pr.buf(use), sc.buf(use)[:, 0:768], ACT.Exp, scale=SCALE).then_inc(sc.sem_free(use), 1)

                if g == 4:
                    values_copy(it, a, s, 0)
                if g == H // 2 - 1:
                    values_copy(it, a, s, 1)

            def values_copy(it, a, s, half):
                use = (("pv", s, half), a)
                act.wait_ge(*pr.released(it, ("st", a, s, 4 * half + 3)))
                if half or s:
                    act.wait_ge(*sc.filled(it, ("vT", a, s, 0) if half else ("vT", a, s - 1, 1)))
                A(xnT[:, :], am.buf(use), ACT.Copy).then_inc(am.sem_free(use), 1)

            def out_copy(it, a):
                use = ("oT", a)
                act.wait_ge(*am.filled(it, use))
                A(xnT[:, :], am.buf(use), ACT.Copy).then_inc(am.sem_free(use), 1)

            def xf_copy(it):
                act.wait_ge(*bb.filled(it, "xfT"))
                A(ynT[:, :], bb.buf("xfT"), ACT.Identity, scale=ln2[:, 0:1]).then_inc(xf_ready.sem, 1)
                A(yhh[:, :], bb.buf("xfT"), ACT.Identity, scale=ln2[:, 0:1]).then_inc(bb.sem_free("xfT"), 1)

            def exp0(it):
                act.wait_ge(*bb.released(it, "router0"))
                A(ro0["ex"][:, :, :], ro0["ex"][:, :, :], ACT.Exp).then_inc(ex0_ready.sem, 1)

            def gelu(it, e):
                act.wait_ge(*bc.filled(it, ("up", e)))
                if e >= 2:
                    act.wait_ge(*bb.filled(it, ("down0", e - 2)))
                A(hid_bufs[e % 2], bc.buf(("up", e)), ACT.Gelu).then_inc(bc.sem_free(("up", e)), 1)

            def yn_copy(it):
                act.wait_ge(*bb.filled(it, "ynT"))
                A(ynT[:, :], bb.buf("ynT"), ACT.Identity, scale=ln_g[:, 0:1], bias=ln_b[:, 0:1])\
                    .then_inc(bb.sem_free("ynT"), 1)

            def u_copy(it):
                act.wait_ge(*bc.filled(it, "u"))
                act.wait_ge(*y_ready.at(it, 0))
                A(upad[:, :, NC - 1:NC - 1 + S], bc.buf("u").rearrange("p (d t) -> p d t", t=S), ACT.Copy)\
                    .then_inc(bc.sem_free("u"), 1)

            def silu_u(it):
                act.wait_ge(*conv_ready.at(it, 1))
                A(u[:, :, :], u[:, :, :], ACT.Silu).then_inc(u_ready.sem, 1)

            def silu_z(it):
                act.wait_ge(*bc.filled(it, "z"))
                A(zs, bc.buf("z").rearrange("p (d t) -> p d t", t=S), ACT.Silu).then_inc(bc.sem_free("z"), 1)

            def split_bc(it):
                act.wait_ge(*bb.filled(it, "dbc"))
                act_steps.note(A(dtin[2 * NS:2 * NS + NDT, :], bb.buf("dbc")[2 * NS:2 * NS + NDT, :], ACT.Copy))
                A(bcp[0:2 * NS, :], bb.buf("dbc")[0:2 * NS, :], ACT.Copy).then_inc(b1_ready.sem, 1)
                act.wait_ge(*bb.released(it, "dbc"))
                A(bc2[:, :], bcr[:, :], ACT.Copy).then_inc(b2_ready.sem, 1)
                A(bcp[2 * NS:4 * NS, :], bcr[:, :], ACT.Copy).then_inc(b2c_ready.sem, 1)

            def softplus_exp(it):
                act.wait_ge(*bc.filled(it, "dt"))
                for d in range(ND):
                    last = A(sp_x[:, d * T:(d + 1) * T], bc.buf("dt")[:, d * T:(d + 1) * T], ACT.Identity,
                             bias=dt_bias[:, d:d + 1])
                last.then_inc(bc.sem_free("dt"), 1)
                act.wait_ge(*bc.released(it, "dt"))
                act_steps.note(A(sp_e, sp_x, ACT.Abs))
                act.wait_ge(*act_steps.now(it))
                A(sp_e, sp_e, ACT.Exp, scale=-1.0).then_inc(spe_ready.sem, 1)

            def softplus_ln(it):
                act.wait_ge(*spw_ready.at(it, 1))
                A(sp_l, sp_w, ACT.Ln).then_inc(spl_ready.sem, 1)

            def b_rows(it, g):
                for d in range(ND if g >= 1 else 0):
                    act.wait_ge(*dbr.filled(it, (g - 1, d)))
                for j in range(2):
                    use = ("B", 2 * g + j)
                    act.wait_ge(*bb.filled(it, use))
                    A(brow[:, j, :], bb.buf(use), ACT.Copy).then_inc(bb.sem_free(use), 1)

            def decays(it, g, d):
                use = (g, d)
                if use == chunks[0]:
                    act.wait_ge(*dt_ready.at(it, 1))
                act.wait_ge(*dar.emptied(it, use))
                for j in range(2):
                    last = A(dar.buf(use)[:, j * T:(j + 1) * T].rearrange("p (s t) -> p s t", s=NSEQ)[:, :, 1:S],
                             dt[:, d, :].rearrange("p (s t) -> p s t", s=NSEQ)[:, :, 1:S],
                             ACT.Exp, scale=decay[:, d, 2 * g + j:2 * g + j + 1])
                last.then_inc(dar.sem_full(use), 1)

            def yh_copy(it):
                act.wait_ge(*bb.filled(it, "yhT"))
                A(ynT[:, :], bb.buf("yhT"), ACT.Copy).then_inc(yhf_ready.sem, 1)
                A(yhh[:, :], bb.buf("yhT"), ACT.Copy).then_inc(bb.sem_free("yhT"), 1)

            def exp1(it):
                act.wait_ge(*lg1_ready.at(it, 1))
                A(ro1["ex"][:, :, :], ro1["ex"][:, :, :], ACT.Exp).then_inc(ex1_ready.sem, 1)

            def g_copy(it):
                act.wait_ge(*bb.filled(it, "gT"))
                A(gT[:, :], bb.buf("gT")[0:E1, :], ACT.Copy).then_inc(bb.sem_free("gT"), 1)

            def tanh(it, e):
                act.wait_ge(*gate_ready.at(it, e + 1))
                if e >= 2:
                    act.wait_ge(*act_ready.at(it, e - 1))
                A(tanh_b[e % 2], gate_b[e % 2], ACT.Tanh, scale=ALPHA / 2).then_inc(tanh_ready.sem, 1)

            def weigh1(it, e):
                use = ("down1", e)
                act.wait_ge(*bb.filled(it, use))
                if e == 0:
                    act.wait_ge(*halved.at(it, 1))
                if e >= 2:
                    act.wait_ge(*acc_added.at(it, e - 1))
                for t in range(NT):
                    last = A(weighed[e % 2][:, t * P:(t + 1) * P], bb.buf(use)[:, t * P:(t + 1) * P], ACT.Copy,
                             scale=half_gates[:, t, e:e + 1])
                last.then_inc(bb.sem_free(use), 1)

            def together(a, b):
                front, back = steps_of(a, b)
                act_steps.begin()
                back(xf_copy)
                front(x_copy, 0)
                back(exp0)
                back(gelu, 0)
                front(first_parts, 0)
                back(gelu, 1)
                front(second_parts, 0)
                for e in range(2, E0):
                    back(gelu, e)
                back(yn_copy)
                back(u_copy)
                back(silu_u)
                back(silu_z)
                front(first_part, 0, 0)
                back(split_bc)
                back(b_rows, 0)
                back(softplus_exp)
                front(first_part, 0, 1)
                front(exponent, 0, 0, 0)
                back(softplus_ln)
                front(exponent, 0, 0, 1)
                back(decays, 0, 0)
                front(exponent, 0, 0, 2)
                back(decays, 0, 1)
                front(exponent, 0, 0, 3)
                front(exponent, 0, 0, 4)
                front(exponent, 0, 0, 5)
                for c, (g, d) in enumerate(chunks):
                    if 1 <= c < len(chunks) - 1:
                        back(decays, *chunks[c + 1])
                    if d == 0 and g + 1 < NCH:
                        back(b_rows, g + 1)
                    for n in SCORES_AT[c]:
                        front(exponent, 0, n // (H // 2), n % (H // 2))
                    if c == OUT_AT:
                        front(out_copy, 0)
                    if c == NEXT_AT:
                        front(x_copy, 1)
                        front(first_parts, 1)
                        front(second_parts, 1)
                back(yh_copy)
                back(exp1)
                back(tanh, 0)
                front(first_part, 1, 0)
                back(g_copy)
                front(first_part, 1, 1)
                for g in range(2):
                    front(exponent, 1, 0, g)
                for e in range(E1):
                    if e >= 1:
                        back(tanh, e)
                        back(weigh1, e - 1)
                    for n in ATTEND_AT[e]:
                        front(exponent, 1, n // (H // 2), n % (H // 2))
                    if e == OUT1_AT:
                        front(out_copy, 1)
                back(weigh1, E1 - 1)
                if b is not None:
                    act_steps.end()

            act.wait_ge(w_load, LOADS)
            A(decay[:, :, :], decay[:, :, :], ACT.Exp).then_inc(w_decay, 1)
            act.wait_ge(w_decay, 1)
            A(decay[:, :, :], decay[:, :, :], ACT.Copy, scale=-1.0).then_inc(w_decay, 1)
            act.wait_ge(w_decay, 2)
            act.wait_ge(w_ready, W_READY)
            together(0, None)
            together(1, 0)
            with act.Fori(1, pairs - 1) as it:
                together(it + 1, it)
            together(None, pairs - 1)

        @block.gpsimd
        def _(pool):
            G = nc.gpsimd.tensor_tensor

            def power(it, k, ve, rstd, var, rstd_s):
                pool.wait_ge(*var.at(it, k + 1))
                G(rstd[:, :], ve[:, :], minus_half[:, :], ALU.pow).then_inc(rstd_s.sem, 1)

            def third_parts(it, a):
                for k, src in enumerate((qf, kf)):
                    pool.wait_ge(*p2_ready.at(it, 2 * a + k + 1))
                    G(parts[:, k, 2, :], src, parts[:, k, 1, :], ALU.subtract).then_inc(p3_ready.sem, 1)

            def power_a(it, k):
                power(it, k, ve_a, rstd_a, var_a, rstd_s_a)

            def add1(it, e):
                pool.wait_ge(*bb.released(it, ("down1", e)))
                if e >= 1:
                    pool.wait_ge(*acc_added.at(it, e))
                G(acc[:, :, :], acc[:, :, :], weighed[e % 2].rearrange("p (t c) -> p t c", c=C), ALU.add)\
                    .then_inc(acc_added.sem, 1)

            def power_b(it, k):
                power(it, k, ve_b, rstd_b, var_b, rstd_s_b)

            def x_bias(it):
                pool.wait_ge(*x_loaded.at(it, 16))
                pool.wait_ge(*acc0_ready.at(it, 0))
                G(x1[:, :, :], xin[:, :, :], bo[:, :].unsqueeze(1).to_broadcast([P, NT, C]), ALU.add)\
                    .then_inc(xbias_ready.sem, 1)

            def residuals(it):
                pool.wait_ge(*am.released(it, ("proj", 1)))
                pool.wait_ge(*base_ready.at(it, 0))
                G(x2[:, :, :], x1[:, :, :], xa[:, :, :], ALU.add).then_inc(acc0_ready.sem, 1)

            def base(it):
                pool.wait_ge(*norm_b.at(it, 2))
                G(xl[:, :, :], x2[:, :, :], xl[:, :, :], ALU.add).then_inc(base_ready.sem, 1)

            def dt_b_u(it, c):
                use = chunks[c]
                g, d = use
                if d == 0:
                    pool.wait_ge(*bb.released(it, ("B", 2 * g + 1)))
                if c >= 2:
                    pool.wait_ge(*dar.released(it, chunks[c - 2]))
                G(dbr.buf(use).rearrange("p (j t) -> p j t", j=2), brow[:, :, :],
                  u[:, d, :].unsqueeze(1).to_broadcast([P, 2, T]), ALU.mult).then_inc(dbr.sem_full(use), 1)

            def add_y(it, c):
                use = chunks[c]
                g, d = use
                pool.wait_ge(*hsr.filled(it, use))
                if g >= 1:
                    pool.wait_ge(*hsr.released(it, chunks[c - 2]))
                h2 = hsr.buf(use).rearrange("p (j t) -> p j t", j=2)
                if g == 0:
                    G(y[:, d, 0, :], y[:, d, 0, :], h2[:, 0, :], ALU.add)
                    ins = nc.gpsimd.tensor_copy(y[:, d, 1, :], h2[:, 1, :])
                else:
                    ins = G(y[:, d, :, :], y[:, d, :, :], h2, ALU.add)
                ins.then_inc(hsr.sem_free(use), 1)

            def together(a, b):
                front, back = steps_of(a, b)
                front(power_a, 0)
                front(x_bias)
                front(third_parts, 0)
                back(power_b, 0)
                back(power_b, 1)
                back(base)
                if b is not None:
                    pool.wait_ge(*dtu_ready.at(b, 1))
                back(dt_b_u, 0)
                for c in range(len(chunks)):
                    if c + 1 < len(chunks) and c + 1 not in DVE_CHUNKS:
                        back(dt_b_u, c + 1)
                    if c == OUT_AT + 2:
                        front(power_a, 1)
                    if c == OUT_AT + 3:
                        front(power_a, 2)
                    back(add_y, c)
                    if c == NEXT_AT:
                        front(third_parts, 1)
                back(power_b, 2)
                for e in range(E1):
                    back(add1, e)
                    if e == OUT1_AT:
                        front(residuals)
                        front(power_a, 3)

            pool.wait_ge(w_load, LOADS)
            pool.wait_ge(w_ready, W_READY)
            together(0, None)
            together(1, 0)
            with pool.Fori(1, pairs - 1) as it:
                together(it + 1, it)
            together(None, pairs - 1)


def _swap_pairs(w):
    return w.reshape(C // 2, 2, -1)[:, ::-1].reshape(w.shape)


def _constants(np):
    pos = np.arange(S, dtype=np.float32)[:, None]
    dim = np.arange(HD // 2, dtype=np.float32)[None, :]
    theta = pos / np.exp(np.float32(2.0) * dim / np.float32(HD) * np.float32(np.log(10000.0)))
    cos, sin = np.cos(theta), np.sin(theta)
    sign = np.array([-1.0, 1.0], np.float32)
    cosT = np.repeat(cos.T, 2, axis=0)
    sinT = np.repeat(sin.T, 2, axis=0) * np.tile(sign, HD // 2)[:, None]
    i = np.arange(P)
    later = i[None, :] > i[:, None]
    one = np.arange(2 * NS)
    return {
        "cos": np.tile(cosT, (H, 1)).astype(np.float32), "sin": np.tile(sinT, (H, 1)).astype(np.float32),
        "ident": np.eye(P, dtype=np.float32),
        "pick": np.tile((one[:, None] == one[None, :]).astype(np.float32), (NPART, 1)),
        "mask_qk": np.where(later, np.float32(NEG), np.float32(0)).astype(np.float32),
        "mask_kq": np.where(later.T, np.float32(NEG), np.float32(0)).astype(np.float32),
        "expert0": np.tile(np.repeat(np.arange(E0, dtype=np.float32), K0), (P, 1)),
        "expert1": np.tile(np.repeat(np.arange(E1, dtype=np.float32), K1), (P, 1)),
        "ones": np.ones((KM - KS, H, T), mybir.dt.np(BF16)),
    }


def kernel(**inputs):
    import numpy as np
    import concourse.bacc as bacc
    from concourse.bass_utils import run_bass_kernel_spmd

    i = {k: np.asarray(v) for k, v in inputs.items()}
    a, f, m, g = "L0_attn_", "L0_ffn_", "L1_attn_", "L1_ffn_"
    x = i[a + "x"]
    n_seq = x.shape[0]
    wx, gub = i[m + "W_x"], i[g + "gate_up_bias"]
    arrays = {
        "x": x.reshape(-1, C),
        "wqT": i[a + "wq"].T, "wqsT": _swap_pairs(i[a + "wq"]).T,
        "wkT": i[a + "wk"].T, "wksT": _swap_pairs(i[a + "wk"]).T,
        "wvT": i[a + "wv"].T, "woT": i[a + "wo"].T,
        "qk_bias": np.stack([i[a + "bq"], _swap_pairs(i[a + "bq"]), i[a + "bk"], _swap_pairs(i[a + "bk"])], axis=1),
        "bv": np.tile(i[a + "bv"], (P, 1)), "bo": np.tile(i[a + "bo"], (P, 1)),
        "ln1": i[f + "ln1_w"][:, None], "ln2": i[f + "ln2_w"][:, None],
        "c_attn": i[f + "c_attn_w"], "c_proj": i[f + "c_proj_w"],
        "router0": i[f + "router_w"], "w1": i[f + "w1"], "w2": i[f + "w2"],
        "ln_g": i[m + "ln_g"][:, None], "ln_b": i[m + "ln_b"][:, None],
        "WinT": i[m + "W_in"].T, "conv_w": i[m + "conv_w"], "conv_b": i[m + "conv_b"].reshape(ND, P).T,
        "WxT": np.concatenate([wx[NDT:], wx[:NDT]]).T, "WdtT": i[m + "W_dt"].T,
        "dt_bias": i[m + "dt_bias"].reshape(ND, P).T, "A_log": i[m + "A_log"], "D": i[m + "D"].reshape(ND, P).T, "WoutT": i[m + "W_out"].T,
        "router1T": i[g + "router_weight"].T, "router_bias": np.tile(i[g + "router_bias"], (P, 1)),
        "gate_up": i[g + "gate_up_proj"],
        "gate_up_biasT": np.concatenate([gub[:, :F1], gub[:, F1:]]).T,
        "down": i[g + "down_proj"], "down_bias": i[g + "down_bias"],
        **_constants(np),
    }
    assert set(arrays) == set(INPUTS)
    nc = bacc.Bacc("TRN2", target_bir_lowering=False, num_devices=1)
    feed, aps = {}, {}
    for name in INPUTS:
        arr = np.ascontiguousarray(arrays[name])
        feed[f"in_{name}"] = arr
        aps[name] = nc.dram_tensor(f"in_{name}", arr.shape, mybir.dt.from_np(arr.dtype), kind="ExternalInput").ap()
    out = nc.dram_tensor("out_y", (n_seq * S, C), F32, kind="ExternalOutput").ap()
    build_program(nc, aps, out, n_seq // NSEQ)
    r = run_bass_kernel_spmd(nc, [feed], core_ids=[0])
    return r.results[0]["out_y"].reshape(n_seq, S, C)
```
